# Optimizing a Trainium2 kernel written in Bass

```python
import numpy as np
import jax
import jax.numpy as jnp

def _softmax(x, axis=-1):
    return jax.nn.softmax(x, axis=axis)

def _gelu(x):
    return jax.nn.gelu(x, approximate=True)

def _silu(x):
    return jax.nn.silu(x)

def _sigmoid(x):
    return jax.nn.sigmoid(x)

def _layernorm(x, axis=-1, eps=1e-05):
    m = jnp.mean(x, axis=axis, keepdims=True)
    v = jnp.var(x, axis=axis, keepdims=True)
    return (x - m) / jnp.sqrt(v + eps)

def _scatter_add(tgt, idx, src, axis=0):
    return tgt.at[idx].add(src)

def _segment_sum(src, seg, n):
    return jax.ops.segment_sum(src, seg, n)
kernel_name = 'mk_adj_seq_d2_adj_r2_18bbc4'

def setup_inputs(seed: int=0):
    np.random.seed(seed)
    _w = jnp.asarray

    def _rec_inputs():
        import jax
        import jax.numpy as jnp
        _gk = jax.random.key(seed)
        x = -0.0002928 + 1 * jax.random.normal(jax.random.fold_in(_gk, 1), (8, 1024, 256), jnp.float32)
        _w = (1.0 + jnp.arange(1024, dtype=jnp.float32)) ** (-0.5)
        _w = _w / _w.mean()
        _pij = jnp.clip(0.00390625 * _w[:, None] * _w[None, :], 0.0, 1.0)
        _a = jax.random.uniform(jax.random.fold_in(_gk, 2), (8, 1024, 1024)) < _pij
        _a = jnp.logical_or(_a, jnp.eye(1024, dtype=bool))
        adj = _a.astype(jnp.int32)
        return (x, adj)
    x, adj = _rec_inputs()

    def _L0_gnn_setup():
        import jax, jax.numpy as jnp
        import numpy as np
        B, N, D, H = (4, 1024, 256, 8)
        HD = D // H
        EPS = 1e-05
        key = jax.random.key(seed)
        ks = jax.random.split(key, 12)
        x = jax.random.normal(ks[0], (B, N, D), dtype=jnp.float32)
        adj = jax.random.randint(ks[1], (B, N, N), 0, 2, dtype=jnp.int32)
        adj = jnp.maximum(adj, jnp.eye(N, dtype=jnp.int32)[None, :, :])
        s = 1.0 / np.sqrt(D)
        Wq = jax.random.uniform(ks[2], (D, D), jnp.float32, -s, s)
        bq = jnp.zeros((D,), jnp.float32)
        Wk = jax.random.uniform(ks[3], (D, D), jnp.float32, -s, s)
        bk = jnp.zeros((D,), jnp.float32)
        Wv = jax.random.uniform(ks[4], (D, D), jnp.float32, -s, s)
        bv = jnp.zeros((D,), jnp.float32)
        Wo = jax.random.uniform(ks[5], (D, D), jnp.float32, -s, s)
        bo = jnp.zeros((D,), jnp.float32)
        gamma = jnp.ones((D,), jnp.float32)
        beta = jnp.zeros((D,), jnp.float32)
        return {'x': x, 'adj': adj, 'Wq': Wq, 'bq': bq, 'Wk': Wk, 'bk': bk, 'Wv': Wv, 'bv': bv, 'Wo': Wo, 'bo': bo, 'gamma': gamma, 'beta': beta}
    _L0_gnn_all = _L0_gnn_setup()
    _L0_gnn_in = {k: v for k, v in _L0_gnn_all.items() if k in ('Wq', 'bq', 'Wk', 'bk', 'Wv', 'bv', 'Wo', 'bo', 'gamma', 'beta')}
    del _L0_gnn_all

    def _L1_gnn_setup():
        import jax, jax.numpy as jnp
        import numpy as np
        B, N, H, D = (8, 512, 256, 4)
        EPS = 1e-08
        LN_EPS = 1e-05

        def _linear(x, W, b):
            return x @ W.T + b
        key = jax.random.key(seed)
        ks = jax.random.split(key, 20)
        inp = {'adj': jax.random.randint(ks[0], (B, N, N), 0, D + 1, dtype=jnp.int32), 'relative_pos': jax.random.randint(ks[1], (B, N, N), 0, 16, dtype=jnp.int32), 'hid': jax.random.normal(ks[2], (B, N, H), dtype=jnp.float32), 'Wd': jax.random.normal(ks[3], (H, D * H), dtype=jnp.float32) * (1.0 / np.sqrt(D * H)), 'bd': jnp.zeros((H,), jnp.float32)}
        s = 1.0 / np.sqrt(H)
        for i, nm in enumerate(['ri', 'rh', 'zi', 'zh', 'ni', 'nh']):
            inp['W' + nm] = jax.random.normal(ks[4 + i], (H, H), dtype=jnp.float32) * s
            inp['b' + nm] = jnp.zeros((H,), jnp.float32)
        inp['gamma'] = jnp.ones((H,), jnp.float32)
        inp['beta'] = jnp.zeros((H,), jnp.float32)
        return inp
    _L1_gnn_all = _L1_gnn_setup()
    _L1_gnn_in = {k: v for k, v in _L1_gnn_all.items() if k in ('Wd', 'bd', 'Wri', 'bri', 'Wrh', 'brh', 'Wzi', 'bzi', 'Wzh', 'bzh', 'Wni', 'bni', 'Wnh', 'bnh', 'gamma', 'beta')}
    del _L1_gnn_all
    return {'x': x, 'adj': adj, 'L0_gnn_Wq': _L0_gnn_in['Wq'], 'L0_gnn_bq': _L0_gnn_in['bq'], 'L0_gnn_Wk': _L0_gnn_in['Wk'], 'L0_gnn_bk': _L0_gnn_in['bk'], 'L0_gnn_Wv': _L0_gnn_in['Wv'], 'L0_gnn_bv': _L0_gnn_in['bv'], 'L0_gnn_Wo': _L0_gnn_in['Wo'], 'L0_gnn_bo': _L0_gnn_in['bo'], 'L0_gnn_gamma': _L0_gnn_in['gamma'], 'L0_gnn_beta': _L0_gnn_in['beta'], 'L1_gnn_Wd': _L1_gnn_in['Wd'], 'L1_gnn_bd': _L1_gnn_in['bd'], 'L1_gnn_Wri': _L1_gnn_in['Wri'], 'L1_gnn_bri': _L1_gnn_in['bri'], 'L1_gnn_Wrh': _L1_gnn_in['Wrh'], 'L1_gnn_brh': _L1_gnn_in['brh'], 'L1_gnn_Wzi': _L1_gnn_in['Wzi'], 'L1_gnn_bzi': _L1_gnn_in['bzi'], 'L1_gnn_Wzh': _L1_gnn_in['Wzh'], 'L1_gnn_bzh': _L1_gnn_in['bzh'], 'L1_gnn_Wni': _L1_gnn_in['Wni'], 'L1_gnn_bni': _L1_gnn_in['bni'], 'L1_gnn_Wnh': _L1_gnn_in['Wnh'], 'L1_gnn_bnh': _L1_gnn_in['bnh'], 'L1_gnn_gamma': _L1_gnn_in['gamma'], 'L1_gnn_beta': _L1_gnn_in['beta']}

def reference(x, adj, L0_gnn_Wq, L0_gnn_bq, L0_gnn_Wk, L0_gnn_bk, L0_gnn_Wv, L0_gnn_bv, L0_gnn_Wo, L0_gnn_bo, L0_gnn_gamma, L0_gnn_beta, L1_gnn_Wd, L1_gnn_bd, L1_gnn_Wri, L1_gnn_bri, L1_gnn_Wrh, L1_gnn_brh, L1_gnn_Wzi, L1_gnn_bzi, L1_gnn_Wzh, L1_gnn_bzh, L1_gnn_Wni, L1_gnn_bni, L1_gnn_Wnh, L1_gnn_bnh, L1_gnn_gamma, L1_gnn_beta):
    import jax
    import jax.numpy as jnp

    def _L0_gnn_ref(x, adj, Wq, bq, Wk, bk, Wv, bv, Wo, bo, gamma, beta):
        import jax, jax.numpy as jnp
        import numpy as np
        B, N, D, H = (4, 1024, 256, 8)
        HD = D // H
        EPS = 1e-05
        b, n, d = x.shape
        scale = 1.0 / np.sqrt(HD).astype(np.float32)
        q = (x @ Wq + bq).reshape(b, n, H, HD)
        k = (x @ Wk + bk).reshape(b, n, H, HD)
        v = (x @ Wv + bv).reshape(b, n, H, HD)
        scores = jnp.einsum('bnhd,bmhd->bhnm', q, k) * scale
        mask = (adj == 0)[:, None, :, :]
        scores = jnp.where(mask, jnp.float32(-jnp.inf), scores)
        attn = jax.nn.softmax(scores, axis=-1)
        h = jnp.einsum('bhnm,bmhd->bnhd', attn, v).reshape(b, n, d)
        h = h @ Wo + bo
        y = h + x
        mu = jnp.mean(y, axis=-1, keepdims=True)
        var = jnp.mean(jnp.square(y - mu), axis=-1, keepdims=True)
        return (y - mu) * jax.lax.rsqrt(var + EPS) * gamma + beta

    def _L1_gnn_ref(adj, relative_pos, hid, Wd, bd, Wri, bri, Wrh, brh, Wzi, bzi, Wzh, bzh, Wni, bni, Wnh, bnh, gamma, beta):
        import jax, jax.numpy as jnp
        import numpy as np
        B, N, H, D = (8, 512, 256, 4)
        EPS = 1e-08
        LN_EPS = 1e-05

        def _linear(x, W, b):
            return x @ W.T + b
        dt = hid.dtype
        labels = jnp.arange(1, D + 1, dtype=adj.dtype)
        mask = (adj[None] == labels[:, None, None, None]).astype(dt)
        weight = mask / (jnp.sum(mask, axis=-1, keepdims=True) + EPS)
        agg = jnp.einsum('dbmn,bnh->bmdh', weight, hid).reshape(hid.shape[0], hid.shape[1], D * H)
        out = jax.nn.relu(_linear(agg, Wd, bd))
        r = jax.nn.sigmoid(_linear(out, Wri, bri) + _linear(hid, Wrh, brh))
        z = jax.nn.sigmoid(_linear(out, Wzi, bzi) + _linear(hid, Wzh, bzh))
        n = jnp.tanh(_linear(out, Wni, bni) + r * _linear(hid, Wnh, bnh))
        out = (1.0 - z) * n + z * hid
        mu = jnp.mean(out, axis=-1, keepdims=True)
        var = jnp.var(out, axis=-1, keepdims=True)
        return (out - mu) / jnp.sqrt(var + LN_EPS) * gamma + beta
    x = _L0_gnn_ref(x, adj, L0_gnn_Wq, L0_gnn_bq, L0_gnn_Wk, L0_gnn_bk, L0_gnn_Wv, L0_gnn_bv, L0_gnn_Wo, L0_gnn_bo, L0_gnn_gamma, L0_gnn_beta)
    x = _L1_gnn_ref(adj, adj, x, L1_gnn_Wd, L1_gnn_bd, L1_gnn_Wri, L1_gnn_bri, L1_gnn_Wrh, L1_gnn_brh, L1_gnn_Wzi, L1_gnn_bzi, L1_gnn_Wzh, L1_gnn_bzh, L1_gnn_Wni, L1_gnn_bni, L1_gnn_Wnh, L1_gnn_bnh, L1_gnn_gamma, L1_gnn_beta)
    return x

_drawn_inputs = setup_inputs


def setup_inputs(seed=0):
    import zlib

    import numpy as np

    out = dict(_drawn_inputs(seed))
    spreads = {'L0_gnn_bq': (0.0, 0.8),
     'L0_gnn_bk': (0.0, 0.8),
     'L0_gnn_bv': (0.0, 0.1),
     'L0_gnn_bo': (0.0, 0.1),
     'L0_gnn_gamma': (1.0, 0.2),
     'L0_gnn_beta': (0.0, 0.1),
     'L1_gnn_bd': (0.0, 0.1),
     'L1_gnn_bri': (0.0, 0.672),
     'L1_gnn_brh': (0.0, 0.607),
     'L1_gnn_bzi': (0.0, 0.1),
     'L1_gnn_bzh': (0.0, 0.1),
     'L1_gnn_bni': (0.0, 0.1),
     'L1_gnn_bnh': (0.0, 0.1),
     'L1_gnn_gamma': (1.0, 0.2),
     'L1_gnn_beta': (0.0, 0.1)}
    factors = {}
    for name, (base, spread) in spreads.items():
        noise = np.random.default_rng([zlib.crc32(name.encode()), seed]).standard_normal(out[name].shape)
        drawn = base * np.exp(spread * noise) if base else spread * noise
        out[name] = jnp.asarray(drawn.astype(out[name].dtype))
    for name, factor in factors.items():
        out[name] = (out[name] * factor).astype(out[name].dtype)
    return out
```

```python
from contextlib import ExitStack

import numpy as np

import concourse.bass as bass
from concourse import mybir

F32 = mybir.dt.float32
F32R = mybir.dt.float32r
BF16 = mybir.dt.bfloat16
I32 = mybir.dt.int32
ALU = mybir.AluOpType
ACT = mybir.ActivationFunctionType
AX = mybir.AxisListType

P = 128
B, N, D, H = 8, 1024, 256, 8
HD = D // H
DC = D // P
NT = N // P
HALF = 512
NH = N // HALF
QUARTERS = 4
LAG = 2
GH = P // HD
G = H // GH
LABELS = 4
KROWS = 3 * HD
SROW = KROWS
SCALE = float(np.float32(1.0) / np.sqrt(HD).astype(np.float32))
EDGE = 2.0 ** 60
NOEDGE = -1.0e30
EPS0 = 1e-5
EPS_COUNT = 1e-8
NEG_INF = -3.0e38
SLOTS = 2
PSLOTS = 3
TILES = NT * H
COLUMNS = ("bq", "bk", "bd", "bri", "brh", "bzi", "bzh", "bni", "bnh")
ALL_01 = N // 4
N_CONST = 18
N_FIN = NT
PAIRS = QUARTERS * NT * 2


def graph_kernel(nc, a, out):
    ctx = ExitStack()
    with ctx:
        def sb(name, shape, dt):
            return ctx.enter_context(nc.sbuf_tensor(name, shape, dt))

        x1_dram = nc.dram_tensor("x1_scratch", (B, N, D), F32, kind="Internal").ap()

        shift_dram = nc.dram_tensor("shift_scratch", (H * NT, P), F32, kind="Internal").ap()

        w0 = {k: sb(f"w_{k}", [P, DC, D], F32) for k in ("q", "k", "v", "o")}
        w1 = {k: sb(f"w_{k}", [P, DC, D], F32) for k in ("ri", "rh", "zi", "zh", "ni", "nh")}
        wd = sb("wd", [P, DC, D], F32)
        cols = sb("cols", [P, len(COLUMNS), DC], F32)
        col = {k: cols[:, i, :] for i, k in enumerate(COLUMNS)}
        row = {k: sb(f"row_{k}", [P, D], F32) for k in ("bv", "bo", "g0", "b0", "g1", "b1")}
        ident = sb("ident", [P, P], F32)
        ones = sb("ones", [P, P], BF16)
        half_power = sb("half_power", [P, NT], F32)

        xT = sb("xT", [P, DC, N], F32)
        x1 = sb("x1", [P, NT, D], F32)
        kst = [sb(f"kst{g}", [P, GH, N], F32R) for g in range(G)]
        qst = [sb(f"qst{g}", [P, GH, N], F32R) for g in range(G)]
        vals = sb("vals", [P, NT, D], F32)
        edge = sb("edge", [P, NT, N], BF16)
        bias = [sb(f"bias{i}", [P, N], BF16) for i in range(2)]
        adj_n = [sb(f"adj_n{i}", [P, N], I32) for i in range(2)]
        adj_t = [sb(f"adj_t{i}", [P, N], I32) for i in range(1)]
        scores = [sb(f"scores{i}", [P, N], F32) for i in range(SLOTS)]
        proj = sb("proj", [P, HALF], F32)
        part_hi, part_lo = (scores[i][:, :].bitcast(F32R) for i in range(2))
        negmax = sb("negmax", [P, H, NT], F32)
        shift_r = sb("shift_r", [P, H, NT], F32R)
        excess = sb("excess", [P, H, NT], F32)
        rowsum = sb("rowsum", [P, H, NT], F32)
        recsum = sb("recsum", [P, H, NT], F32)
        shift = sb("shift", [H * NT, P], F32)
        recb = sb("recb", [P, HALF], F32)
        more = sb("more", [P, NT], F32)
        more_any = sb("more_any", [P, NT], F32)
        stats = sb("stats", [P, 2, 6], F32)
        mv = sb("mv", [P, NT, 2], F32)
        rstd = sb("rstd", [P, NT], F32)
        small = sb("small", [P, NT], F32)
        stats2 = sb("stats2", [P, 2, 6], F32)
        mv2 = sb("mv2", [P, 4, 2], F32)
        rstd2 = sb("rstd2", [P, 4], F32)
        small2 = sb("small2", [P, 4], F32)
        minus_half = sb("minus_half", [P, 1], F32)
        flag = sb("flag", [P, 1], F32)
        flags = sb("flags", [P, 2], BF16)
        general_flag = sb("general_flag", [1, 1], I32)

        ground = sb("ground", [P, 14 * HALF], F32)
        probs = [ground[:, i * 2048:(i + 1) * 2048].rearrange("p (h n) -> p h n", h=GH)
                 for i in range(PSLOTS)]

        def area(i, n):
            return ground[:, i * HALF:(i + n) * HALF]

        x1T = area(0, 2).rearrange("p (c n) -> p c n", c=DC)
        aggT = area(2, 4).rearrange("p (c n) -> p c n", c=DC)
        outT = area(6, 2).rearrange("p (c n) -> p c n", c=DC)
        rT = area(8, 2).rearrange("p (c n) -> p c n", c=DC)
        zT = area(10, 2).rearrange("p (c n) -> p c n", c=DC)
        nT = area(12, 2).rearrange("p (c n) -> p c n", c=DC)
        rest = area(8, 4).rearrange("p (t d) -> p t d", t=NT)
        turned = sb("turned", [P, DC * N], F32)
        hT = turned[:, :].rearrange("p (c n) -> p c n", c=DC)
        x1a = turned[:, 0:N].bitcast(BF16).rearrange("p (t d) -> p t d", t=NT)
        x1b = turned[:, N:2 * N].bitcast(BF16).rearrange("p (t d) -> p t d", t=NT)
        x1c = sb("x1c", [P, NT, D], BF16)
        recip = proj
        final = sb("final", [P, 4, D], F32)

        label_adj = [buf[:, :, :].bitcast(I32).rearrange("p a b -> p (a b)").rearrange("p (k n) -> p k n", k=NT // 2)
                     for buf in (xT, vals)]
        label_mask = edge[:, :, :].bitcast(F32)
        label_wd = turned[:, :].rearrange("p (k n) -> p k n", k=LABELS * DC)
        ones_f = w0["q"][:, 0, 0:P]

        SP = [ctx.enter_context(nc.psum_tensor(f"SP{i}", [P, N], F32)) for i in range(2)]
        GB = [ctx.enter_context(nc.psum_tensor(f"GB{i}", [P, HALF], F32)) for i in range(4)]

        names = """xT_in x1_in adjn_in0 adjn_in1 adjt_in
            proj_ps proj_sb hi_made lo_made stack_moved vals_ps vals_sb bias_made edge_made more_read
            score_ps score_sb exp_made shift_ps shift_sb shift_moved recsum_made shift_rounded excess_made excess_exp sum_shifted
            st_ps prob_made prob_masked pv_done att_ps att_sb rec_ps rec_sb biased
            y_ps y_sum mv_made eps_added rstd_made normed scaled x1_made x1a_made rest_made x1b_made x1c_made x1_saved
            x1T_ps x1T_sb cnt_ps cnt_sum recip_made agg_ps agg_sb wd_ps out_sb
            r_ps z_ps ni_ps nh_ps rt_made zt_made r_made t_made s_made n_made diff_made prod_made new_made
            fin_ps st2_made mv2_made eps2_added rstd2_made fin_normed fin_scaled fin_made fin_saved
            stats_made more_made shift_out
            wd_part wd_in labels_in ones_made mask_made""".split()

        def bc(ap, shape):
            return ap.unsqueeze(1).broadcast_to(shape)

        const_in, ident_zero, const_pool, const_vec = (
            nc.alloc_semaphore(n) for n in ("const_in", "ident_zero", "const_pool", "const_vec"))
        with nc.Block() as block:
            @block.sync
            def _(sp):
                for k, w in (*w0.items(), *w1.items()):
                    sp.dma_start(w[:, :, :], a["W" + k].rearrange("(c p) n -> p c n", p=P)).then_inc(const_in, 16)
                sp.dma_start(wd[:, :, :], a["Wd"][0:D, :].rearrange("(c p) n -> p c n", p=P)).then_inc(const_in, 16)
                sp.dma_start(cols[:, :, :], a["columns"]).then_inc(const_in, 16)
                for k, r in row.items():
                    sp.dma_start(r[:, :], a[k].partition_broadcast(P)).then_inc(const_in, 16)

            @block.vector
            def _(dve):
                dve.memset(more_any[:, :], -float(B * ALL_01))
                dve.memset(minus_half[:, :], -0.5)
                for g in range(G):
                    dve.memset(kst[g][SROW:SROW + 1, :, :].bitcast(F32), 1.0)
                dve.wait_ge(const_in, 16 * N_CONST)
                dve.tensor_scalar(col["bq"][:, :], col["bq"][:, :], SCALE, None, ALU.mult)
                for k in "rz":
                    dve.tensor_tensor(col[f"b{k}i"][:, :], col[f"b{k}i"][:, :], col[f"b{k}h"][:, :], ALU.add).then_inc(const_vec, 1)
                dve.wait_ge(const_vec, 2)
                for k in "rz":
                    dve.tensor_scalar(col[f"b{k}i"][:, :], col[f"b{k}i"][:, :], 0.5, None, ALU.mult)

            @block.gpsimd
            def _(pool):
                pool.memset(ident[:, :], 0.0).then_inc(ident_zero, 1)
                pool.memset(ones[:, :], 1.0)
                pool.memset(half_power[:, :], -0.5)
                pool.wait_ge(ident_zero, 1)
                pool.affine_select(out=ident[:, :], in_=ident[:, :], compare_op=ALU.not_equal, fill=1.0, base=0,
                                   pattern=[[-1, P]], channel_multiplier=1)

        nc.clear_and_free_semaphores([const_in, ident_zero, const_pool, const_vec])
        nc.all_engine_barrier()

        def step(b, update, prepare, general=0):
            s = {n: nc.alloc_semaphore(f"{n}_{update}{prepare}{general}") for n in names}
            labels = LABELS if general else 1

            ctx_step = ExitStack()
            block = ctx_step.enter_context(nc.Block())

            @block.sync
            def _(sp):
                def move_part(n, g, k):
                    stack = (qst, kst)[k][g]
                    part = 2 * g + k + 1
                    sp.wait_ge(s["hi_made"], 2 * part)
                    sp.wait_ge(s["lo_made"], 2 * part)
                    for h in range(GH):
                        for r, src in ((0, part_hi), (1, (part_lo, part_hi)[k]), (2, (part_hi, part_lo)[k])):
                            sp.dma_start(stack[r * HD:(r + 1) * HD, h, :].bitcast(F32),
                                         src[h * HD:(h + 1) * HD, :].bitcast(F32)).then_inc(s["stack_moved"], 16)

                def load_xT(b):
                    sp.dma_start(xT[:, :, :], a["xT"][b].rearrange("(c p) n -> p c n", p=P)).then_inc(s["xT_in"], 16)

                def load_adj(n, i):
                    if i > 1:
                        sp.wait_ge(s["bias_made"], i - 1)
                    sp.dma_start(adj_n[i % 2][:, :], a["adj"][n, i * P:(i + 1) * P, :]).then_inc(s[f"adjn_in{i % 2}"], 16)

                def load_adjT(n, i):
                    if i > 0:
                        sp.wait_ge(s["more_read"], i)
                    sp.dma_start(adj_t[0][:, :], a["adjT"][n, i * P:(i + 1) * P, :]).then_inc(s["adjt_in"], 16)

                def phase_a(b, more_to_come):
                    sp.dma_start(x1[:, :, :], a["x"][b].rearrange("(t p) d -> p t d", p=P)).then_inc(s["x1_in"], 16)
                    if more_to_come:
                        load_xT(b + 1)
                        for i in range(2):
                            load_adj(b + 1, i)
                        sp.wait_ge(s["st_ps"], PAIRS // 2)
                        for k in range(2):
                            move_part(b + 1, 0, k)

                def phase_b(b, update, prepare):
                    if not prepare:
                        return
                    n = b + 1
                    if not update:
                        load_xT(0)
                        for i in range(2):
                            load_adj(0, i)
                        for k in range(2):
                            move_part(0, 0, k)
                    for k in range(2):
                        move_part(n, 1, k)
                    for i in range(2, 6):
                        load_adj(n, i)
                    load_adjT(n, 0)
                    for i in range(6, NT):
                        load_adj(n, i)
                    for i in range(1, NT):
                        load_adjT(n, i)
                    sp.wait_ge(s["shift_sb"], 1)
                    sp.dma_start(shift_dram, shift[:, :]).then_inc(s["shift_out"], 16)
                    sp.wait_ge(s["shift_out"], 16)
                    for g in range(G):
                        sp.dma_start(qst[g][SROW:SROW + 1, :, :].bitcast(F32),
                                     shift_dram[g * GH * NT:(g + 1) * GH * NT, :].rearrange("(o h t) n -> o h (t n)", o=1, h=GH)
                                     ).then_inc(s["shift_moved"], 16)

                def load_labels():
                    sp.dma_start(x1[:, :, :], x1_dram[b].rearrange("(t p) d -> p t d", p=P)).then_inc(s["x1_in"], 16)
                    sp.dma_start(label_wd, a["Wd"].rearrange("(k p) n -> p k n", p=P)).then_inc(s["wd_in"], 16)
                    for mh in range(NH):
                        if mh > 0:
                            sp.wait_ge(s["mask_made"], 2 * LABELS * mh)
                        for e in range(2):
                            sp.dma_start(label_adj[e], a["adjT"][b, e * N // 2:(e + 1) * N // 2, mh * HALF:(mh + 1) * HALF]
                                         .rearrange("(k p) n -> p k n", p=P)).then_inc(s["labels_in"], 16)

                if general:
                    load_labels()
                elif update:
                    phase_a(b, prepare)
                phase_b(b, update, prepare)
                if prepare:
                    sp.wait_ge(s["shift_moved"], 32)

            @block.tensor
            def _(pe):
                def project(n, i):
                    g, k, nh = i // 4, i // 2 % 2, i % 2
                    if i == 0:
                        pe.wait_ge(s["xT_in"], 16)
                    if i > 0:
                        pe.wait_ge(s["proj_sb"], i)
                    for c in range(DC):
                        last = pe.matmul(GB[2][:, :], w0["qk"[k]][:, c, g * P:(g + 1) * P],
                                         xT[:, c, nh * HALF:(nh + 1) * HALF], start=(c == 0), stop=(c == DC - 1))
                    last.then_inc(s["proj_ps"], 1)

                def values(n, i):
                    if i == 0 and update:
                        pe.wait_ge(s["prob_made"], PAIRS)
                    for t in range(2):
                        for c in range(DC):
                            last = pe.matmul(SP[i // 2][:, (i % 2 * 2 + t) * D:(i % 2 * 2 + t + 1) * D], xT[:, c, (2 * i + t) * P:(2 * i + t + 1) * P],
                                             w0["v"][:, c, :], start=(c == 0), stop=(c == DC - 1))
                    last.then_inc(s["vals_ps"], 1)

                def phase_a(b, more_to_come):
                    for q in range(QUARTERS * NT + LAG):
                        j, t = q // NT, q % NT
                        if j < QUARTERS:
                            g, nh = j // NH, j % NH
                            for hp in range(2):
                                p = 2 * q + hp
                                if p >= 2:
                                    pe.wait_ge(s["prob_made"], p - 1)
                                for e in range(2):
                                    h = 2 * hp + e
                                    last = pe.matmul(SP[p % 2][:, e * HALF:(e + 1) * HALF],
                                                     kst[g][0:SROW + 1, h, t * P:(t + 1) * P],
                                                     qst[g][0:SROW + 1, h, nh * HALF:(nh + 1) * HALF],
                                                     start=True, stop=True)
                                last.then_inc(s["st_ps"], 1)
                        if q >= LAG:
                            w = q - LAG
                            k, tw = w // NT, w % NT
                            pe.wait_ge(s["prob_masked"], 2 * (w + 1))
                            if tw == 0 and k >= 2:
                                pe.wait_ge(s["att_sb"], k - 1)
                            for h in range(GH):
                                f = k // NH * P + h * HD
                                last = pe.matmul(GB[k % 2][h * HD:(h + 1) * HD, :], vals[:, tw, f:f + HD],
                                                 probs[w % PSLOTS][:, h, :], start=(tw == 0), stop=(tw == NT - 1))
                            last.then_inc(s["pv_done"], 1)
                        if t == 4:
                            if j > 0:
                                pe.wait_ge(s["rec_sb"], j)
                            for i in range(4):
                                for h in range(GH):
                                    last = pe.matmul(GB[3][h * HD:(h + 1) * HD, i * P:(i + 1) * P],
                                                     recsum[:, g * GH + h, nh * 4 + i:nh * 4 + i + 1].broadcast_to([P, HD]),
                                                     ident[:, :], start=True, stop=True)
                            last.then_inc(s["rec_ps"], 1)
                        if more_to_come and j == 2 and t % 2 == 1:
                            project(b + 1, t // 2)

                def phase_b(b, update, prepare):
                    n = b + 1
                    done = [0]

                    def score_tiles(count):
                        if not prepare:
                            return
                        for u in range(done[0], done[0] + count):
                            t, h = u // H, u % H
                            if u < 2:
                                pe.wait_ge(s["vals_sb"], 2 * u + 2)
                            if u == 0:
                                pe.wait_ge(s["stack_moved"], 16 * 48)
                                if update:
                                    pe.wait_ge(s["prob_made"], PAIRS)
                            if u >= 2:
                                pe.wait_ge(s["score_sb"], u - 1)
                            for mh in range(NH):
                                last = pe.matmul(SP[u % 2][:, mh * HALF:(mh + 1) * HALF],
                                                 qst[h // GH][0:KROWS, h % GH, t * P:(t + 1) * P],
                                                 kst[h // GH][0:KROWS, h % GH, mh * HALF:(mh + 1) * HALF],
                                                 start=True, stop=True)
                            last.then_inc(s["score_ps"], 1)
                        done[0] += count

                    if not update:
                        for i in range(4):
                            project(n, i)
                    for i in range(4):
                        if prepare:
                            project(n, 4 + i)
                        if update and not general:
                            if i == 0:
                                pe.wait_ge(s["att_sb"], 4)
                            if i >= 2:
                                pe.wait_ge(s["y_sum"], i - 1)
                            for t in range(2):
                                for c in range(DC):
                                    last = pe.matmul(GB[i % 2][:, t * D:(t + 1) * D], hT[:, c, (2 * i + t) * P:(2 * i + t + 1) * P],
                                                     w0["o"][:, c, :], start=(c == 0), stop=(c == DC - 1))
                            last.then_inc(s["y_ps"], 1)
                    if prepare:
                        for i in range(4):
                            values(n, i)
                    score_tiles(24)
                    if update and not general:
                        pe.wait_ge(s["x1c_made"], 2)
                        pe.wait_ge(s["x1b_made"], 2)
                        pe.wait_ge(s["y_sum"], 4)
                        if prepare:
                            pe.wait_ge(s["vals_sb"], 4)
                        else:
                            pe.wait_ge(s["rec_sb"], 4)
                    for mh in range(0 if general else NH):
                        cols = slice(mh * HALF, (mh + 1) * HALF)
                        if update:
                            for k in range(NT):
                                last = pe.matmul(GB[mh][:, :], ones[:, :], edge[:, k, cols], start=(k == 0), stop=(k == NT - 1))
                            last.then_inc(s["cnt_ps"], 1)
                        for dh in range(DC):
                            if update and mh == 1:
                                pe.wait_ge(s["agg_sb"], dh + 1)
                            for k in range(NT):
                                if update:
                                    for e, part in enumerate((x1a, x1b, x1c)):
                                        last = pe.matmul(GB[2 + dh][:, :], part[:, k, dh * P:(dh + 1) * P], edge[:, k, cols],
                                                         start=(k == 0 and e == 0), stop=(k == NT - 1 and e == 2))
                                if k % 2 == 1:
                                    score_tiles(1)
                            if update:
                                last.then_inc(s["agg_ps"], 1)
                    for mh in range(NH):
                        if update:
                            if mh == 0:
                                pe.wait_ge(s["recip_made"], 2 * labels)
                                if general:
                                    pe.wait_ge(s["x1_in"], 16)
                                else:
                                    pe.wait_ge(s["x1_made"], 2)
                            else:
                                pe.wait_ge(s["fin_normed"], NT // 2)
                            for dh in range(DC):
                                for t in range(4):
                                    last = pe.transpose(GB[dh][:, t * P:(t + 1) * P], x1[:, 4 * mh + t, dh * P:(dh + 1) * P], ident[:, :])
                                last.then_inc(s["x1T_ps"], 1)
                        score_tiles(3)
                        if update and mh == 0:
                            pe.wait_ge(s["agg_sb"], 4 * labels)
                        if update and not general:
                            for oh in range(DC):
                                for c in range(DC):
                                    last = pe.matmul(GB[2 + oh][:, :], wd[:, c, oh * P:(oh + 1) * P],
                                                     aggT[:, c, mh * HALF:(mh + 1) * HALF], start=(c == 0), stop=(c == DC - 1))
                                last.then_inc(s["wd_ps"], 1)
                        score_tiles(3)
                        for oh in range(DC):
                            if mh == 1 and oh == 0:
                                score_tiles(3)
                            q = 2 * mh + oh
                            o = slice(oh * P, (oh + 1) * P)

                            def gate(bank, inner, outer, signal):
                                pairs = [(w1[inner], outT, c) for c in range(DC)] if inner else []
                                pairs += [(w1[outer], x1T, c) for c in range(DC)] if outer else []
                                for m, (w, v, c) in enumerate(pairs):
                                    last = pe.matmul(GB[bank][:, :], w[:, c, o], v[:, c, :], start=(m == 0), stop=(m == len(pairs) - 1))
                                last.then_inc(s[signal], 1)

                            if update:
                                if oh == 0:
                                    pe.wait_ge(s["x1T_sb"], 2 * (mh + 1))
                                    pe.wait_ge(s["out_sb"], 2 * (mh + 1))
                                if q > 0:
                                    pe.wait_ge(s["rt_made"], q)
                                gate(0, "ri", "rh", "r_ps")
                                if q > 0:
                                    pe.wait_ge(s["zt_made"], q)
                                gate(1, "zi", "zh", "z_ps")
                                if q > 0:
                                    pe.wait_ge(s["t_made"], q)
                                gate(3, None, "nh", "nh_ps")
                                if q > 0:
                                    pe.wait_ge(s["s_made"], q)
                                gate(2, "ni", None, "ni_ps")
                            if mh == 0:
                                score_tiles(3)
                            elif oh == 0 and prepare:
                                pe.wait_ge(s["shift_rounded"], 1)
                                pe.transpose(SP[0][0:H * NT, 0:P], shift_r[:, :, :].bitcast(F32).rearrange("p h t -> p (h t)"),
                                             ident[:, :]).then_inc(s["shift_ps"], 1)
                        if mh == 0:
                            score_tiles(3)
                        if update:
                            pe.wait_ge(s["new_made"], 2 * (mh + 1))
                            for k in range(2):
                                for t in range(2):
                                    for oh in range(DC):
                                        last = pe.transpose(GB[k][:, t * D + oh * P:t * D + (oh + 1) * P],
                                                            nT[:, oh, (2 * k + t) * P:(2 * k + t + 1) * P], ident[:, :])
                                last.then_inc(s["fin_ps"], 1)

                def label_sums():
                    pe.wait_ge(s["x1_in"], 16)
                    pe.wait_ge(s["ones_made"], 1)
                    pe.wait_ge(s["wd_in"], 16)
                    for mh in range(NH):
                        for d in range(LABELS):
                            r = LABELS * mh + d
                            pe.wait_ge(s["mask_made"], 2 * (r + 1))
                            if r > 0:
                                pe.wait_ge(s["cnt_sum"], r)
                            for k in range(NT):
                                last = pe.matmul(GB[0][:, :], ones_f, label_mask[:, k, :], start=(k == 0), stop=(k == NT - 1))
                            last.then_inc(s["cnt_ps"], 1)
                            if r > 0:
                                pe.wait_ge(s["agg_sb"], DC * r)
                            for dh in range(DC):
                                for k in range(NT):
                                    last = pe.matmul(GB[2 + dh][:, :], x1[:, k, dh * P:(dh + 1) * P], label_mask[:, k, :],
                                                     start=(k == 0), stop=(k == NT - 1))
                                last.then_inc(s["agg_ps"], 1)
                            pe.wait_ge(s["agg_sb"], DC * (r + 1))
                            for oh in range(DC):
                                for c in range(DC):
                                    last = pe.matmul(SP[mh][:, oh * HALF:(oh + 1) * HALF], label_wd[:, DC * d + c, oh * P:(oh + 1) * P],
                                                     aggT[:, c, mh * HALF:(mh + 1) * HALF], start=(d == 0 and c == 0),
                                                     stop=(d == LABELS - 1 and c == DC - 1))
                                if d == LABELS - 1:
                                    last.then_inc(s["wd_ps"], 1)
                                elif oh == DC - 1:
                                    last.then_inc(s["wd_part"], 1)

                if general:
                    label_sums()
                elif update:
                    phase_a(b, prepare)
                phase_b(b, update, prepare)

            @block.scalar
            def _(act):
                def project(n, i):
                    g, k = i // 4, i // 2 % 2
                    act.wait_ge(s["proj_ps"], i + 1)
                    if i > 0:
                        act.wait_ge(s["lo_made"], i)
                    if i > 0:
                        act.wait_ge(s["hi_made"], i)
                    act.activation(proj[:, :], GB[2][:, :], ACT.Identity, bias=col[("bq", "bk")[k]][:, g:g + 1],
                                   scale=(SCALE, 1.0)[k]).then_inc(s["proj_sb"], 1)

                def phase_a(b, more_to_come):
                    for j in range(QUARTERS):
                        for t in range(NT):
                            q = j * NT + t
                            if q >= PSLOTS:
                                act.wait_ge(s["pv_done"], q - PSLOTS + 1)
                            for hp in range(2):
                                p = 2 * q + hp
                                act.wait_ge(s["st_ps"], p + 1)
                                act.activation(probs[q % PSLOTS][:, 2 * hp:2 * hp + 2, :],
                                               SP[p % 2][:, :].rearrange("p (h n) -> p h n", h=2), ACT.Exp).then_inc(s["prob_made"], 1)
                            if t == 5:
                                act.wait_ge(s["rec_ps"], j + 1)
                                if j > 0:
                                    act.wait_ge(s["att_sb"], j)
                                act.activation(recb[:, :], GB[3][:, :], ACT.Copy).then_inc(s["rec_sb"], 1)
                            if more_to_come and j == 2 and t % 2 == 1:
                                project(b + 1, t // 2)

                def phase_b(b, update, prepare):
                    n = b + 1
                    done = [0]

                    def score_tiles(count):
                        if not prepare:
                            return
                        for u in range(done[0], done[0] + count):
                            t, h = u // H, u % H
                            act.wait_ge(s["score_sb"], u + 1)
                            act.activation(scores[u % SLOTS][:, :], scores[u % SLOTS][:, :], ACT.Exp, scale=-1.0,
                                           bias=negmax[:, h, t:t + 1], accum_out=rowsum[:, h, t:t + 1]).then_inc(s["exp_made"], 1)
                        done[0] += count

                    def look_through(i):
                        if prepare:
                            act.wait_ge(s["edge_made"], i + 1)
                            act.activation(adj_t[0][:, :], adj_t[0][:, :], ACT.Square, bias=minus_half[:, :], accum_out=more[:, i:i + 1]).then_inc(s["more_read"], 1)

                    if not update:
                        for i in range(4):
                            project(n, i)
                    if prepare:
                        for i in range(4):
                            project(n, 4 + i)
                    score_tiles(14)
                    if update and not general:
                        for e in range(2):
                            half = slice(4 * e, 4 * e + 4)
                            act.wait_ge(s["x1_made"], e + 1)
                            act.wait_ge(s["att_sb"], 4)
                            act.wait_ge(s["y_ps"], 4)
                            act.activation(x1a[:, half, :], x1[:, half, :], ACT.Copy).then_inc(s["x1a_made"], 1)
                    score_tiles(5)
                    if update and not general:
                        for e in range(2):
                            half = slice(4 * e, 4 * e + 4)
                            act.wait_ge(s["rest_made"], e + 1)
                            act.activation(x1b[:, half, :], rest[:, half, :], ACT.Copy).then_inc(s["x1b_made"], 1)
                    score_tiles(5)
                    score_tiles(16)
                    for mh in range(NH):
                        if update:
                            for dh in range(DC):
                                act.wait_ge(s["x1T_ps"], 2 * mh + dh + 1)
                                if mh == 1:
                                    act.wait_ge(s["new_made"], 2)
                                act.activation(x1T[:, dh, :], GB[dh][:, :], ACT.Copy).then_inc(s["x1T_sb"], 1)
                        score_tiles(3)
                        if mh == 0:
                            look_through(0)
                            look_through(1)
                        if update:
                            for oh in range(DC):
                                act.wait_ge(s["wd_ps"], 2 * mh + oh + 1)
                                product = SP[mh][:, oh * HALF:(oh + 1) * HALF] if general else GB[2 + oh][:, :]
                                act.activation(outT[:, oh, :], product, ACT.Relu, bias=col["bd"][:, oh:oh + 1]).then_inc(s["out_sb"], 1)
                        score_tiles(3)
                        if mh == 0:
                            look_through(2)
                            look_through(3)
                        for oh in range(DC):
                            if mh == 1 and oh == 0 and prepare:
                                score_tiles(3)
                                act.wait_ge(s["excess_made"], 1)
                                act.activation(excess[:, :, :], excess[:, :, :], ACT.Exp).then_inc(s["excess_exp"], 1)
                            q = 2 * mh + oh
                            if update:
                                act.wait_ge(s["r_ps"], q + 1)
                                if mh == 0 and oh == 0 and not general:
                                    act.wait_ge(s["x1c_made"], 2)
                                act.activation(rT[:, oh, :], GB[0][:, :], ACT.Tanh, bias=col["bri"][:, oh:oh + 1], scale=0.5).then_inc(s["rt_made"], 1)
                                act.wait_ge(s["z_ps"], q + 1)
                                act.activation(zT[:, oh, :], GB[1][:, :], ACT.Tanh, bias=col["bzi"][:, oh:oh + 1], scale=0.5).then_inc(s["zt_made"], 1)
                            if mh == 0:
                                score_tiles(3)
                                look_through(4 + 2 * oh)
                                look_through(5 + 2 * oh)
                            if update:
                                act.wait_ge(s["s_made"], q + 1)
                                act.activation(nT[:, oh, :], nT[:, oh, :], ACT.Tanh, bias=col["bni"][:, oh:oh + 1]).then_inc(s["n_made"], 1)
                        if mh == 0:
                            score_tiles(3)

                if update and not general:
                    phase_a(b, prepare)
                phase_b(b, update, prepare)

            @block.vector
            def _(dve):
                def high_part(n, i):
                    part = i // 2
                    dve.wait_ge(s["proj_sb"], i + 1)
                    if i % 2 == 0:
                        if part > 0:
                            dve.wait_ge(s["stack_moved"], 16 * 12 * part)
                    cols = slice(i % 2 * HALF, (i % 2 + 1) * HALF)
                    dve.tensor_copy(part_hi[:, cols], proj[:, :]).then_inc(s["hi_made"], 1)

                def phase_a(b, more_to_come):
                    def normalise(j):
                        g, nh = j // NH, j % NH
                        dve.wait_ge(s["pv_done"], NT * (j + 1))
                        dve.wait_ge(s["rec_sb"], j + 1)
                        dve.tensor_tensor(hT[:, g, nh * HALF:(nh + 1) * HALF], GB[j % 2][:, :], recb[:, :], ALU.mult).then_inc(s["att_sb"], 1)

                    for j in range(QUARTERS):
                        for t in range(NT):
                            for hp in range(2):
                                p = (j * NT + t) * 2 + hp
                                dve.wait_ge(s["prob_made"], p + 1)
                                tile = probs[(j * NT + t) % PSLOTS][:, 2 * hp:2 * hp + 2, :]
                                dve.tensor_tensor(tile, tile, bc(edge[:, t, j % NH * HALF:(j % NH + 1) * HALF], [P, 2, HALF]),
                                                  ALU.min).then_inc(s["prob_masked"], 1)
                            if j > 0 and t == 3:
                                normalise(j - 1)
                            if more_to_come and j == 2 and t % 2 == 1:
                                high_part(b + 1, t // 2)
                    normalise(QUARTERS - 1)

                def phase_b(b, update, prepare):
                    n = b + 1
                    done = [0]

                    def score_tiles(count):
                        if not prepare:
                            return
                        for u in range(done[0], done[0] + count):
                            t, h = u // H, u % H
                            if h == 0:
                                dve.wait_ge(s[f"adjn_in{t % 2}"], 16 * (t // 2 + 1))
                                if u > H:
                                    dve.wait_ge(s["score_sb"], u - H)
                                dve.tensor_scalar(bias[t % 2][:, :], adj_n[t % 2][:, :], 0.0, NOEDGE,
                                                  ALU.is_equal, ALU.mult).then_inc(s["bias_made"], 1)
                                dve.wait_ge(s["bias_made"], t + 1)
                            dve.wait_ge(s["score_ps"], u + 1)
                            if u >= SLOTS:
                                dve.wait_ge(s["exp_made"], u - SLOTS + 1)
                            dve.tensor_tensor_reduce(out=scores[u % SLOTS][:, :], in0=SP[u % 2][:, :], in1=bias[t % 2][:, :],
                                                     scale=-1.0, scalar=-NEG_INF, op0=ALU.add, op1=ALU.min,
                                                     accum_out=negmax[:, h, t:t + 1]).then_inc(s["score_sb"], 1)
                        done[0] += count

                    def combine(q):
                        oh = q % 2
                        dve.wait_ge(s["n_made"], q + 1)
                        dve.tensor_tensor(rT[:, oh, :], x1T[:, oh, :], nT[:, oh, :], ALU.subtract).then_inc(s["diff_made"], 1)
                        dve.wait_ge(s["diff_made"], q + 1)
                        dve.scalar_tensor_tensor(rT[:, oh, :], zT[:, oh, :], 1.0, rT[:, oh, :], ALU.add, ALU.mult).then_inc(s["prod_made"], 1)
                        dve.wait_ge(s["prod_made"], q + 1)
                        dve.scalar_tensor_tensor(nT[:, oh, :], rT[:, oh, :], 0.5, nT[:, oh, :], ALU.mult, ALU.add).then_inc(s["new_made"], 1)

                    def edges(i):
                        if prepare:
                            dve.wait_ge(s["adjt_in"], 16 * (i + 1))
                            if i == 0:
                                if update:
                                    dve.wait_ge(s["agg_ps"], 4)
                                if update:
                                    dve.wait_ge(s["cnt_ps"], 2)
                            dve.tensor_scalar(edge[:, i, :], adj_t[0][:, :], 0.0, EDGE, ALU.not_equal, ALU.mult).then_inc(s["edge_made"], 1)

                    if not update:
                        for i in range(4):
                            high_part(n, i)
                    for i in range(4):
                        if prepare:
                            high_part(n, 4 + i)
                        if update and not general:
                            two = slice(2 * i, 2 * i + 2)
                            dve.wait_ge(s["y_ps"], i + 1)
                            dve.wait_ge(s["biased"], 1)
                            dve.tensor_tensor(x1[:, two, :], GB[i % 2][:, :].rearrange("p (t d) -> p t d", t=2), x1[:, two, :],
                                              ALU.add).then_inc(s["y_sum"], 1)
                            dve.wait_ge(s["y_sum"], i + 1)
                            if i > 0:
                                dve.wait_ge(s["mv_made"], 2 * i)
                            for t in range(2):
                                dve.bn_stats(stats[:, t, :], x1[:, 2 * i + t, :]).then_inc(s["stats_made"], 1)
                            for t in range(2):
                                dve.wait_ge(s["stats_made"], 2 * i + t + 1)
                                dve.bn_aggr(mv[:, 2 * i + t, :], stats[:, t, :]).then_inc(s["mv_made"], 1)
                    if prepare:
                        for i in range(4):
                            dve.wait_ge(s["vals_ps"], i + 1)
                            dve.tensor_tensor(vals[:, 2 * i:2 * i + 2, :], SP[i // 2][:, i % 2 * HALF:(i % 2 + 1) * HALF].rearrange("p (t d) -> p t d", t=2),
                                              bc(row["bv"][:, :], [P, 2, D]), ALU.add).then_inc(s["vals_sb"], 1)
                    score_tiles(4)
                    if update and not general:
                        dve.wait_ge(s["rstd_made"], 1)
                        for t in range(NT):
                            dve.tensor_scalar(x1[:, t, :], x1[:, t, :], mv[:, t, 0:1], rstd[:, t:t + 1],
                                              ALU.subtract, ALU.mult).then_inc(s["normed"], 1)
                    score_tiles(20)
                    for mh in range(0 if general else NH):
                        if update:
                            dve.wait_ge(s["cnt_ps"], mh + 1)
                            if mh > 0:
                                dve.wait_ge(s["agg_sb"], 2 * mh)
                            dve.tensor_scalar(recip[:, :], GB[mh][:, :], EDGE * EPS_COUNT, None, ALU.add).then_inc(s["cnt_sum"], 1)
                            dve.wait_ge(s["cnt_sum"], mh + 1)
                            dve.reciprocal(recip[:, :], recip[:, :]).then_inc(s["recip_made"], 1)
                        for dh in range(DC):
                            score_tiles(4)
                            if update:
                                dve.wait_ge(s["agg_ps"], 2 * mh + dh + 1)
                                dve.wait_ge(s["recip_made"], mh + 1)
                                dve.tensor_tensor(aggT[:, dh, mh * HALF:(mh + 1) * HALF], GB[2 + dh][:, :], recip[:, :],
                                                  ALU.mult).then_inc(s["agg_sb"], 1)
                    for mh in range(NH):
                        score_tiles(3)
                        if mh == 0:
                            edges(0)
                            edges(1)
                        score_tiles(3)
                        if mh == 0:
                            edges(2)
                            edges(3)
                        for oh in range(DC):
                            if mh == 1 and oh == 0 and prepare:
                                score_tiles(3)
                                dve.wait_ge(s["score_sb"], TILES)
                                dve.tensor_copy(shift_r[:, :, :], negmax[:, :, :]).then_inc(s["shift_rounded"], 1)
                                dve.wait_ge(s["shift_rounded"], 1)
                                dve.tensor_tensor(excess[:, :, :], shift_r[:, :, :].bitcast(F32), negmax[:, :, :],
                                                  ALU.subtract).then_inc(s["excess_made"], 1)
                            if mh == 0:
                                score_tiles(3)
                                edges(4 + 2 * oh)
                                edges(5 + 2 * oh)
                            q = 2 * mh + oh
                            if update:
                                dve.wait_ge(s["nh_ps"], q + 1)
                                dve.wait_ge(s["rt_made"], q + 1)
                                dve.tensor_scalar(rT[:, oh, :], rT[:, oh, :], 0.5, 0.5, ALU.mult, ALU.add).then_inc(s["r_made"], 1)
                                if mh == 0 and oh == 1:
                                    combine(0)
                                dve.wait_ge(s["r_made"], q + 1)
                                dve.scalar_tensor_tensor(nT[:, oh, :], GB[3][:, :], col["bnh"][:, oh:oh + 1], rT[:, oh, :],
                                                         ALU.add, ALU.mult).then_inc(s["t_made"], 1)
                                dve.wait_ge(s["ni_ps"], q + 1)
                                dve.wait_ge(s["t_made"], q + 1)
                                dve.tensor_tensor(nT[:, oh, :], GB[2][:, :], nT[:, oh, :], ALU.add).then_inc(s["s_made"], 1)
                        if mh == 0:
                            score_tiles(3)
                        if update:
                            for q in ((1,), (2, 3))[mh]:
                                combine(q)
                        if mh == 1 and prepare:
                            dve.wait_ge(s["shift_ps"], 1)
                            dve.tensor_copy(shift[:, :], SP[0][0:H * NT, 0:P]).then_inc(s["shift_sb"], 1)
                            dve.wait_ge(s["exp_made"], TILES)
                            dve.wait_ge(s["excess_exp"], 1)
                            dve.tensor_tensor(rowsum[:, :, :], rowsum[:, :, :], excess[:, :, :], ALU.mult).then_inc(s["sum_shifted"], 1)
                            dve.wait_ge(s["sum_shifted"], 1)
                            if update:
                                dve.wait_ge(s["rec_ps"], 4)
                            dve.reciprocal(recsum[:, :, :], rowsum[:, :, :]).then_inc(s["recsum_made"], 1)
                            dve.wait_ge(s["more_read"], NT)
                            dve.tensor_tensor(more_any[:, :], more_any[:, :], more[:, :], ALU.add).then_inc(s["more_made"], 1)
                        if update:
                            for k in range(2):
                                dve.wait_ge(s["fin_ps"], 2 * mh + k + 1)
                                if mh + k > 0:
                                    dve.wait_ge(s["mv2_made"], 4 * mh + 2 * k)
                                for t in range(2):
                                    dve.bn_stats(stats2[:, t, :], GB[k][:, t * D:(t + 1) * D]).then_inc(s["st2_made"], 1)
                                for t in range(2):
                                    dve.wait_ge(s["st2_made"], 4 * mh + 2 * k + t + 1)
                                    dve.bn_aggr(mv2[:, 2 * k + t, :], stats2[:, t, :]).then_inc(s["mv2_made"], 1)
                            dve.wait_ge(s["rstd2_made"], mh + 1)
                            if mh > 0:
                                dve.wait_ge(s["fin_saved"], 16 * mh)
                            for t in range(4):
                                dve.tensor_scalar(final[:, t, :], GB[t // 2][:, t % 2 * D:(t % 2 + 1) * D], mv2[:, t, 0:1], rstd2[:, t:t + 1],
                                                  ALU.subtract, ALU.mult).then_inc(s["fin_normed"], 1)

                def label_masks():
                    dve.memset(ones_f, 1.0).then_inc(s["ones_made"], 1)
                    for mh in range(NH):
                        for d in range(LABELS):
                            r = LABELS * mh + d
                            dve.wait_ge(s["labels_in"], 32 * (mh + 1))
                            if r > 0:
                                dve.wait_ge(s["agg_ps"], DC * r)
                            if r > 0:
                                dve.wait_ge(s["cnt_ps"], r)
                            for e in range(2):
                                dve.tensor_scalar(label_mask[:, e * NT // 2:(e + 1) * NT // 2, :], label_adj[e], float(d + 1), None,
                                                  ALU.is_equal).then_inc(s["mask_made"], 1)
                            dve.wait_ge(s["cnt_ps"], r + 1)
                            if r > 0:
                                dve.wait_ge(s["agg_sb"], DC * r)
                            dve.tensor_scalar(recip[:, :], GB[0][:, :], EPS_COUNT, None, ALU.add).then_inc(s["cnt_sum"], 1)
                            dve.wait_ge(s["cnt_sum"], r + 1)
                            dve.reciprocal(recip[:, :], recip[:, :]).then_inc(s["recip_made"], 1)
                            dve.wait_ge(s["recip_made"], r + 1)
                            if d > 0:
                                dve.wait_ge(s["wd_part"], (LABELS - 1) * mh + d)
                            for dh in range(DC):
                                dve.wait_ge(s["agg_ps"], DC * r + dh + 1)
                                dve.tensor_tensor(aggT[:, dh, mh * HALF:(mh + 1) * HALF], GB[2 + dh][:, :], recip[:, :],
                                                  ALU.mult).then_inc(s["agg_sb"], 1)

                if general:
                    label_masks()
                elif update:
                    phase_a(b, prepare)
                phase_b(b, update, prepare)

            @block.gpsimd
            def _(pool):
                def low_part(n, i):
                    part = i // 2
                    pool.wait_ge(s["hi_made"], i + 1)
                    if i % 2 == 0:
                        if part > 0:
                            pool.wait_ge(s["stack_moved"], 16 * 12 * part)
                    cols = slice(i % 2 * HALF, (i % 2 + 1) * HALF)
                    pool.tensor_tensor(part_lo[:, cols], proj[:, :], part_hi[:, cols].bitcast(F32), ALU.subtract).then_inc(s["lo_made"], 1)

                def phase_a(b, more_to_come):
                    pool.wait_ge(s["x1_in"], 16)
                    pool.tensor_tensor(x1[:, :, :], x1[:, :, :], bc(row["bo"][:, :], [P, NT, D]), ALU.add).then_inc(s["biased"], 1)
                    if more_to_come:
                        for i in range(4):
                            low_part(b + 1, i)

                def attend(b):
                    pool.wait_ge(s["mv_made"], NT)
                    pool.tensor_scalar(small[:, :], mv[:, :, 1], EPS0, None, ALU.add).then_inc(s["eps_added"], 1)
                    pool.wait_ge(s["eps_added"], 1)
                    pool.tensor_tensor(rstd[:, :], small[:, :], half_power[:, :], ALU.pow).then_inc(s["rstd_made"], 1)
                    for e in range(2):
                        half = slice(4 * e, 4 * e + 4)
                        pool.wait_ge(s["normed"], 4 * (e + 1))
                        pool.tensor_tensor(x1[:, half, :], x1[:, half, :], bc(row["g0"][:, :], [P, 4, D]), ALU.mult).then_inc(s["scaled"], 1)
                        pool.wait_ge(s["scaled"], e + 1)
                        pool.tensor_tensor(x1[:, half, :], x1[:, half, :], bc(row["b0"][:, :], [P, 4, D]), ALU.add).then_inc(s["x1_made"], 1)
                    pool.wait_ge(s["x1_made"], 2)
                    pool.dma_start(x1_dram[b].rearrange("(t p) d -> p t d", p=P), x1[:, :, :]).then_inc(s["x1_saved"], 16)
                    for e in range(2):
                        half = slice(4 * e, 4 * e + 4)
                        pool.wait_ge(s["x1a_made"], e + 1)
                        pool.wait_ge(s["pv_done"], QUARTERS * NT)
                        pool.tensor_tensor(rest[:, half, :], x1[:, half, :], x1a[:, half, :], ALU.subtract).then_inc(s["rest_made"], 1)
                    for e in range(2):
                        half = slice(4 * e, 4 * e + 4)
                        pool.wait_ge(s["x1b_made"], e + 1)
                        pool.tensor_tensor(x1c[:, half, :], rest[:, half, :], x1b[:, half, :], ALU.subtract).then_inc(s["x1c_made"], 1)

                def phase_b(b, update, prepare):
                    n = b + 1
                    if not update:
                        for i in range(4):
                            low_part(n, i)
                    if prepare:
                        for i in range(4):
                            low_part(n, 4 + i)
                    if not update:
                        return
                    if not general:
                        attend(b)
                    for mh in range(NH):
                        pool.wait_ge(s["mv2_made"], 4 * (mh + 1))
                        pool.tensor_scalar(small2[:, :], mv2[:, :, 1], EPS0, None, ALU.add).then_inc(s["eps2_added"], 1)
                        pool.wait_ge(s["eps2_added"], mh + 1)
                        pool.tensor_tensor(rstd2[:, :], small2[:, :], half_power[:, 0:4], ALU.pow).then_inc(s["rstd2_made"], 1)
                        pool.wait_ge(s["fin_normed"], 4 * (mh + 1))
                        pool.tensor_tensor(final[:, :, :], final[:, :, :], bc(row["g1"][:, :], [P, 4, D]), ALU.mult).then_inc(s["fin_scaled"], 1)
                        pool.wait_ge(s["fin_scaled"], mh + 1)
                        pool.tensor_tensor(final[:, :, :], final[:, :, :], bc(row["b1"][:, :], [P, 4, D]), ALU.add).then_inc(s["fin_made"], 1)
                        pool.wait_ge(s["fin_made"], mh + 1)
                        pool.dma_start(out[b, mh * HALF:(mh + 1) * HALF, :].rearrange("(t p) d -> p t d", p=P),
                                       final[:, :, :]).then_inc(s["fin_saved"], 16)

                if update and not general:
                    phase_a(b, prepare)
                phase_b(b, update, prepare)
                if update:
                    pool.wait_ge(s["fin_saved"], 16 * NH)
                if update and not general:
                    pool.wait_ge(s["x1_saved"], 16)


            ctx_step.close()
            nc.clear_and_free_semaphores(list(s.values()))
            nc.all_engine_barrier()

        step(-1, 0, 1)
        with nc.Fori(0, B - 1) as b:
            step(b, 1, 1)
        step(B - 1, 1, 0)

        flag_made, flag_ps, flag_sb, flag_read = (nc.alloc_semaphore(n) for n in ("flag_made", "flag_ps", "flag_sb", "flag_read"))
        with nc.Block() as block:
            @block.vector
            def _(dve):
                dve.tensor_reduce(flag[:, :], more_any[:, :], AX.X, ALU.max).then_inc(flag_made, 1)
                dve.wait_ge(flag_made, 1)
                dve.tensor_scalar(flags[:, :], flag[:, :].broadcast_to([P, 2]), 0.0, None, ALU.is_gt).then_inc(flag_made, 1)
                dve.wait_ge(flag_ps, 1)
                dve.tensor_scalar(general_flag[:, :], SP[0][0:1, 0:1], 0.0, None, ALU.is_gt).then_inc(flag_sb, 1)

            @block.tensor
            def _(pe):
                pe.wait_ge(flag_made, 2)
                pe.matmul(SP[0][:, 0:2], ones[:, :], flags[:, :], start=True, stop=True).then_inc(flag_ps, 1)

        nc.clear_and_free_semaphores([flag_made, flag_ps, flag_sb, flag_read])
        nc.all_engine_barrier()
        general = nc.values_load(general_flag[0:1, 0:1], min_val=0, max_val=1)
        with nc.If(general > 0):
            with nc.Fori(0, B) as b:
                step(b, 1, 0, general=1)


_NAMES = {"Wq": "L0_gnn_Wq", "Wk": "L0_gnn_Wk", "Wv": "L0_gnn_Wv", "Wo": "L0_gnn_Wo",
          "bv": "L0_gnn_bv", "bo": "L0_gnn_bo",
          "g0": "L0_gnn_gamma", "b0": "L0_gnn_beta", "g1": "L1_gnn_gamma", "b1": "L1_gnn_beta"}
_COLUMNS = ("L0_gnn_bq", "L0_gnn_bk", "L1_gnn_bd", "L1_gnn_bri", "L1_gnn_brh", "L1_gnn_bzi",
            "L1_gnn_bzh", "L1_gnn_bni", "L1_gnn_bnh")
_TURNED = {"Wd": "L1_gnn_Wd", "Wri": "L1_gnn_Wri", "Wrh": "L1_gnn_Wrh", "Wzi": "L1_gnn_Wzi",
           "Wzh": "L1_gnn_Wzh", "Wni": "L1_gnn_Wni", "Wnh": "L1_gnn_Wnh"}


def kernel(**inputs):
    import numpy as _np
    import concourse.bacc as _bacc
    from concourse import mybir as _mybir
    from concourse.bass_utils import run_bass_kernel_spmd as _run

    laid = {"x": _np.ascontiguousarray(inputs["x"]), "adj": _np.ascontiguousarray(inputs["adj"]),
            "xT": _np.ascontiguousarray(_np.asarray(inputs["x"]).transpose(0, 2, 1)),
            "adjT": _np.ascontiguousarray(_np.asarray(inputs["adj"]).transpose(0, 2, 1))}
    for k, v in _NAMES.items():
        laid[k] = _np.ascontiguousarray(inputs[v])
    for k, v in _TURNED.items():
        laid[k] = _np.ascontiguousarray(_np.asarray(inputs[v]).T)
    columns = _np.stack([_np.asarray(inputs[v]).reshape(DC, P) for v in _COLUMNS])
    laid["columns"] = _np.ascontiguousarray(columns.transpose(2, 0, 1))

    nc = _bacc.Bacc("TRN2", target_bir_lowering=False, num_devices=1)
    aps = {k: nc.dram_tensor(f"in_{k}", v.shape, _mybir.dt.from_np(v.dtype), kind="ExternalInput").ap()
           for k, v in laid.items()}
    out = nc.dram_tensor("out", (B, N, D), _mybir.dt.float32, kind="ExternalOutput").ap()
    graph_kernel(nc, aps, out)
    r = _run(nc, [{f"in_{k}": v for k, v in laid.items()}], core_ids=[0])
    return r.results[0]["out"]
```

```python
from contextlib import ExitStack

import numpy as np

import concourse.bass as bass
from concourse import mybir

F32 = mybir.dt.float32
F32R = mybir.dt.float32r
BF16 = mybir.dt.bfloat16
I32 = mybir.dt.int32
ALU = mybir.AluOpType
ACT = mybir.ActivationFunctionType
AX = mybir.AxisListType

P = 128
B, N, D, H = 8, 1024, 256, 8
HD = D // H
DC = D // P
NT = N // P
HALF = 512
NH = N // HALF
QUARTERS = 4
LAG = 2
GH = P // HD
G = H // GH
LABELS = 4
KROWS = 3 * HD
SROW = KROWS
SCALE = float(np.float32(1.0) / np.sqrt(HD).astype(np.float32))
EDGE = 2.0 ** 60
NOEDGE = -1.0e30
EPS0 = 1e-5
EPS_COUNT = 1e-8
NEG_INF = -3.0e38
SLOTS = 2
PSLOTS = 3
TILES = NT * H
COLUMNS = ("bq", "bk", "bd", "bri", "brh", "bzi", "bzh", "bni", "bnh")
ALL_01 = N // 4
N_CONST = 18
N_FIN = NT
PAIRS = QUARTERS * NT * 2


def graph_kernel(nc, a, out):
    ctx = ExitStack()
    with ctx:
        def sb(name, shape, dt):
            return ctx.enter_context(nc.sbuf_tensor(name, shape, dt))

        x1_dram = nc.dram_tensor("x1_scratch", (B, N, D), F32, kind="Internal").ap()

        shift_dram = nc.dram_tensor("shift_scratch", (H * NT, P), F32, kind="Internal").ap()

        w0 = {k: sb(f"w_{k}", [P, DC, D], F32) for k in ("q", "k", "v", "o")}
        w1 = {k: sb(f"w_{k}", [P, DC, D], F32) for k in ("ri", "rh", "zi", "zh", "ni", "nh")}
        wd = sb("wd", [P, DC, D], F32)
        cols = sb("cols", [P, len(COLUMNS), DC], F32)
        col = {k: cols[:, i, :] for i, k in enumerate(COLUMNS)}
        row = {k: sb(f"row_{k}", [P, D], F32) for k in ("bv", "bo", "g0", "b0", "g1", "b1")}
        ident = sb("ident", [P, P], F32)
        ones = sb("ones", [P, P], BF16)
        half_power = sb("half_power", [P, NT], F32)

        xT = sb("xT", [P, DC, N], F32)
        x1 = sb("x1", [P, NT, D], F32)
        kst = [sb(f"kst{g}", [P, GH, N], F32R) for g in range(G)]
        qst = [sb(f"qst{g}", [P, GH, N], F32R) for g in range(G)]
        vals = sb("vals", [P, NT, D], F32)
        edge = sb("edge", [P, NT, N], BF16)
        bias = [sb(f"bias{i}", [P, N], BF16) for i in range(2)]
        adj_n = [sb(f"adj_n{i}", [P, N], I32) for i in range(2)]
        adj_t0 = sb("adj_t", [P, N], I32)
        scores = [sb(f"scores{i}", [P, N], F32) for i in range(SLOTS)]
        recip = sb("recip", [P, N], F32)
        counts = sb("counts", [P, NT], F32)
        scores_r = [scores[i][:, :].bitcast(F32R) for i in range(2)]
        negmax = sb("negmax", [P, H, NT], F32)
        shift_r = sb("shift_r", [P, H, NT], F32R)
        excess = sb("excess", [P, H, NT], F32)
        rowsum = sb("rowsum", [P, H, NT], F32)
        recsum = sb("recsum", [P, H, NT], F32)
        shift = sb("shift", [H * NT, P], F32)
        recb = recip[:, 0:HALF]
        more = sb("more", [P, NT], F32)
        more_any = sb("more_any", [P, NT], F32)
        stats = sb("stats", [P, 2, 6], F32)
        mv = sb("mv", [P, NT, 2], F32)
        rstd = sb("rstd", [P, NT], F32)
        small = sb("small", [P, NT], F32)
        stats2 = sb("stats2", [P, 2, 6], F32)
        mv2 = sb("mv2", [P, 4, 2], F32)
        rstd2 = sb("rstd2", [P, 4], F32)
        small2 = sb("small2", [P, 4], F32)
        minus_half = sb("minus_half", [P, 1], F32)
        flag = sb("flag", [P, 1], F32)
        flags = sb("flags", [P, 2], BF16)
        general_flag = sb("general_flag", [1, 1], I32)

        ground = sb("ground", [P, 14 * HALF], F32)
        probs = [ground[:, i * 2048:(i + 1) * 2048].rearrange("p (h n) -> p h n", h=GH)
                 for i in range(PSLOTS)]

        def area(i, n):
            return ground[:, i * HALF:(i + n) * HALF]

        x1T = area(0, 2).rearrange("p (c n) -> p c n", c=DC)
        aggT = area(2, 4).rearrange("p (c n) -> p c n", c=DC)
        outT = area(6, 2).rearrange("p (c n) -> p c n", c=DC)
        rT = area(8, 2).rearrange("p (c n) -> p c n", c=DC)
        zT = area(10, 2).rearrange("p (c n) -> p c n", c=DC)
        nT = area(12, 2).rearrange("p (c n) -> p c n", c=DC)
        rest = area(8, 4).rearrange("p (t d) -> p t d", t=NT)
        turned = sb("turned", [P, DC * N], F32)
        hT = turned[:, :].rearrange("p (c n) -> p c n", c=DC)
        x1a = turned[:, 0:N].bitcast(BF16).rearrange("p (t d) -> p t d", t=NT)
        x1b = turned[:, N:2 * N].bitcast(BF16).rearrange("p (t d) -> p t d", t=NT)
        x1c = sb("x1c", [P, NT, D], BF16)
        final = sb("final", [P, 4, D], F32)

        def whole(buf, dt):
            return buf[:, :, :].bitcast(dt).rearrange("p a b -> p (a b)")

        lows = [scores[1][:, :], whole(x1c, F32)]
        lows_r = [scores_r[1], whole(x1c, F32R)]
        highs_r = [scores_r[0], adj_t0[:, :].bitcast(F32R)]

        adj_t = [adj_t0[:, :], whole(x1c, I32)] + [turned[:, e * N:(e + 1) * N].bitcast(I32) for e in range(2)]

        label_adj = [buf[:, :, :].bitcast(I32).rearrange("p a b -> p (a b)").rearrange("p (k n) -> p k n", k=NT // 2)
                     for buf in (xT, vals)]
        label_mask = edge[:, :, :].bitcast(F32)
        label_wd = turned[:, :].rearrange("p (k n) -> p k n", k=LABELS * DC)
        ones_f = w0["q"][:, 0, 0:P]

        SP = [ctx.enter_context(nc.psum_tensor(f"SP{i}", [P, N], F32)) for i in range(2)]
        GB = [ctx.enter_context(nc.psum_tensor(f"GB{i}", [P, HALF], F32)) for i in range(4)]

        names = """xT_in x1_in adjn_in0 adjn_in1 adjt_in0 adjt_in1 adjt_in2 adjt_in3
            proj_ps proj_sb hi_made lo_made stack_moved0 stack_moved1 vals_ps vals_sb bias_made edge_made more_read
            score_ps score_sb exp_made shift_ps shift_sb shift_moved recsum_made shift_rounded excess_made excess_exp sum_shifted
            st_ps prob_made prob_masked pv_done att_ps att_sb rec_ps rec_sb biased
            y_ps y_sum mv_made eps_added rstd_made normed scaled x1_made x1a_made rest_made x1b_made x1c_made x1_saved
            x1T_ps x1T_sb cnt_ps cnt_sum recip_made recip_ps recip_sb agg_ps agg_sb wd_ps out_sb
            r_ps z_ps ni_ps nh_ps rt_made zt_made r_made t_made s_made n_made diff_made prod_made new_made
            fin_ps st2_made mv2_made eps2_added rstd2_made fin_normed fin_scaled fin_made fin_saved
            stats_made more_made shift_out
            wd_part wd_in labels_in ones_made mask_made""".split()

        def bc(ap, shape):
            return ap.unsqueeze(1).broadcast_to(shape)

        const_in, ident_zero, const_pool, const_vec = (
            nc.alloc_semaphore(n) for n in ("const_in", "ident_zero", "const_pool", "const_vec"))
        with nc.Block() as block:
            @block.sync
            def _(sp):
                for k, w in (*w0.items(), *w1.items()):
                    sp.dma_start(w[:, :, :], a["W" + k].rearrange("(c p) n -> p c n", p=P)).then_inc(const_in, 16)
                sp.dma_start(wd[:, :, :], a["Wd"][0:D, :].rearrange("(c p) n -> p c n", p=P)).then_inc(const_in, 16)
                sp.dma_start(cols[:, :, :], a["columns"]).then_inc(const_in, 16)
                for k, r in row.items():
                    sp.dma_start(r[:, :], a[k].partition_broadcast(P)).then_inc(const_in, 16)

            @block.vector
            def _(dve):
                dve.memset(more_any[:, :], -float(B * ALL_01))
                dve.memset(minus_half[:, :], -0.5)
                for g in range(G):
                    dve.memset(kst[g][SROW:SROW + 1, :, :].bitcast(F32), 1.0)
                dve.wait_ge(const_in, 16 * N_CONST)
                dve.tensor_scalar(col["bq"][:, :], col["bq"][:, :], SCALE, None, ALU.mult)
                for k in "rz":
                    dve.tensor_tensor(col[f"b{k}i"][:, :], col[f"b{k}i"][:, :], col[f"b{k}h"][:, :], ALU.add).then_inc(const_vec, 1)
                dve.wait_ge(const_vec, 2)
                for k in "rz":
                    dve.tensor_scalar(col[f"b{k}i"][:, :], col[f"b{k}i"][:, :], 0.5, None, ALU.mult)

            @block.gpsimd
            def _(pool):
                pool.memset(ident[:, :], 0.0).then_inc(ident_zero, 1)
                pool.memset(ones[:, :], 1.0)
                pool.memset(half_power[:, :], -0.5)
                pool.wait_ge(ident_zero, 1)
                pool.affine_select(out=ident[:, :], in_=ident[:, :], compare_op=ALU.not_equal, fill=1.0, base=0,
                                   pattern=[[-1, P]], channel_multiplier=1)

        nc.clear_and_free_semaphores([const_in, ident_zero, const_pool, const_vec])
        nc.all_engine_barrier()

        def step(b, update, prepare, before=0, after=0, general=0):
            s = {n: nc.alloc_semaphore(f"{n}_{update}{prepare}{before}{general}") for n in names}
            labels = LABELS if general else 1

            ctx_step = ExitStack()
            block = ctx_step.enter_context(nc.Block())

            @block.sync
            def _(sp):
                def move_part(g, k):
                    stack = (qst, kst)[k][g]
                    part = 2 * g + k + 1
                    hi, lo = highs_r[k], lows_r[k]
                    sp.wait_ge(s["hi_made"], 2 * part)
                    sp.wait_ge(s["lo_made"], 2 * part)
                    for h in range(GH):
                        for r, src in ((0, hi), (1, (lo, hi)[k]), (2, (hi, lo)[k])):
                            sp.dma_start(stack[r * HD:(r + 1) * HD, h, :].bitcast(F32),
                                         src[h * HD:(h + 1) * HD, :].bitcast(F32)).then_inc(s[f"stack_moved{k}"], 16)

                def load_xT(b):
                    sp.dma_start(xT[:, :, :], a["xT"][b].rearrange("(c p) n -> p c n", p=P)).then_inc(s["xT_in"], 16)

                def load_adj(n, i):
                    if i > 1:
                        sp.wait_ge(s["bias_made"], i - 1)
                    sp.dma_start(adj_n[i % 2][:, :], a["adj"][n, i * P:(i + 1) * P, :]).then_inc(s[f"adjn_in{i % 2}"], 16)

                def load_adjT(n, i):
                    if i == 0:
                        for k in range(2):
                            sp.wait_ge(s[f"stack_moved{k}"], 16 * 24)
                    if i == 1:
                        if update:
                            sp.wait_ge(s["agg_ps"], 4)
                    if i >= 4:
                        sp.wait_ge(s["more_read"], i - 3)
                    sp.dma_start(adj_t[i % 4], a["adjT"][n, i * P:(i + 1) * P, :]).then_inc(s[f"adjt_in{i % 4}"], 16)

                def phase_a(b, more_to_come):
                    sp.dma_start(x1[:, :, :], a["x"][b].rearrange("(t p) d -> p t d", p=P)).then_inc(s["x1_in"], 16)
                    if more_to_come:
                        load_xT(b + 1)
                        for i in range(2):
                            load_adj(b + 1, i)
                        sp.wait_ge(s["st_ps"], PAIRS // 2)
                        for k in range(2):
                            move_part(0, k)
                        sp.wait_ge(s["st_ps"], PAIRS)
                        for k in range(2):
                            move_part(1, k)

                def phase_b(b, update, prepare):
                    if not prepare:
                        return
                    n = b + 1
                    if not update:
                        load_xT(0)
                        for i in range(2):
                            load_adj(0, i)
                        for g in range(G):
                            for k in range(2):
                                move_part(g, k)
                    for i in range(2, 7):
                        load_adj(n, i)
                    for i in range(4):
                        load_adjT(n, i)
                    load_adj(n, 7)
                    for i in range(4, NT):
                        load_adjT(n, i)
                    sp.wait_ge(s["shift_sb"], 1)
                    sp.dma_start(shift_dram, shift[:, :]).then_inc(s["shift_out"], 16)
                    sp.wait_ge(s["shift_out"], 16)
                    for g in range(G):
                        sp.dma_start(qst[g][SROW:SROW + 1, :, :].bitcast(F32),
                                     shift_dram[g * GH * NT:(g + 1) * GH * NT, :].rearrange("(o h t) n -> o h (t n)", o=1, h=GH)
                                     ).then_inc(s["shift_moved"], 16)

                def load_labels():
                    sp.dma_start(x1[:, :, :], x1_dram[b].rearrange("(t p) d -> p t d", p=P)).then_inc(s["x1_in"], 16)
                    sp.dma_start(label_wd, a["Wd"].rearrange("(k p) n -> p k n", p=P)).then_inc(s["wd_in"], 16)
                    for mh in range(NH):
                        if mh > 0:
                            sp.wait_ge(s["mask_made"], 2 * LABELS * mh)
                        for e in range(2):
                            sp.dma_start(label_adj[e], a["adjT"][b, e * N // 2:(e + 1) * N // 2, mh * HALF:(mh + 1) * HALF]
                                         .rearrange("(k p) n -> p k n", p=P)).then_inc(s["labels_in"], 16)

                if general:
                    load_labels()
                elif update:
                    phase_a(b, prepare)
                phase_b(b, update, prepare)
                if prepare:
                    sp.wait_ge(s["shift_moved"], 32)

            @block.tensor
            def _(pe):
                def project(n, i):
                    g, k, nh = i // 4, i // 2 % 2, i % 2
                    if i == 0:
                        pe.wait_ge(s["xT_in"], 16)
                    if i > 0:
                        pe.wait_ge(s["proj_sb"], i)
                    for c in range(DC):
                        last = pe.matmul(GB[2][:, :], w0["qk"[k]][:, c, g * P:(g + 1) * P],
                                         xT[:, c, nh * HALF:(nh + 1) * HALF], start=(c == 0), stop=(c == DC - 1))
                    last.then_inc(s["proj_ps"], 1)

                def values(n, i):
                    if i == 0 and update:
                        pe.wait_ge(s["prob_made"], PAIRS)
                    for t in range(2):
                        for c in range(DC):
                            last = pe.matmul(SP[i // 2][:, (i % 2 * 2 + t) * D:(i % 2 * 2 + t + 1) * D], xT[:, c, (2 * i + t) * P:(2 * i + t + 1) * P],
                                             w0["v"][:, c, :], start=(c == 0), stop=(c == DC - 1))
                    last.then_inc(s["vals_ps"], 1)

                def finish(f, banks):
                    for k, bank in enumerate(banks):
                        for t in range(2):
                            for oh in range(DC):
                                last = pe.transpose(GB[bank][:, t * D + oh * P:t * D + (oh + 1) * P],
                                                    nT[:, oh, (2 * k + t) * P:(2 * k + t + 1) * P], ident[:, :])
                        last.then_inc(s["fin_ps"], 1)

                def phase_a(b, more_to_come):
                    for q in range(QUARTERS * NT + LAG):
                        j, t = q // NT, q % NT
                        if j < QUARTERS:
                            g, nh = j // NH, j % NH
                            for hp in range(2):
                                p = 2 * q + hp
                                if p >= 2:
                                    pe.wait_ge(s["prob_made"], p - 1)
                                for e in range(2):
                                    h = 2 * hp + e
                                    last = pe.matmul(SP[p % 2][:, e * HALF:(e + 1) * HALF],
                                                     kst[g][0:SROW + 1, h, t * P:(t + 1) * P],
                                                     qst[g][0:SROW + 1, h, nh * HALF:(nh + 1) * HALF],
                                                     start=True, stop=True)
                                last.then_inc(s["st_ps"], 1)
                        if q >= LAG:
                            w = q - LAG
                            k, tw = w // NT, w % NT
                            pe.wait_ge(s["prob_masked"], 2 * (w + 1))
                            if tw == 0 and k >= 2:
                                pe.wait_ge(s["att_sb"], k - 1)
                            if tw == 0 and k == 1 and before:
                                pe.wait_ge(s["fin_normed"], 4)
                            for h in range(GH):
                                f = k // NH * P + h * HD
                                last = pe.matmul(GB[k % 2][h * HD:(h + 1) * HD, :], vals[:, tw, f:f + HD],
                                                 probs[w % PSLOTS][:, h, :], start=(tw == 0), stop=(tw == NT - 1))
                            last.then_inc(s["pv_done"], 1)
                        if t == 4:
                            if j > 0:
                                pe.wait_ge(s["rec_sb"], j)
                            for i in range(4):
                                for h in range(GH):
                                    last = pe.matmul(GB[3][h * HD:(h + 1) * HD, i * P:(i + 1) * P],
                                                     recsum[:, g * GH + h, nh * 4 + i:nh * 4 + i + 1].broadcast_to([P, HD]),
                                                     ident[:, :], start=True, stop=True)
                            last.then_inc(s["rec_ps"], 1)
                        if before and q == 4:
                            finish(0, (1, 2))
                        if more_to_come and j in (2, 3) and t % 2 == 1:
                            project(b + 1, 4 * (j - 2) + t // 2)

                def turn_x1(mh):
                    for dh in range(DC):
                        for t in range(4):
                            last = pe.transpose(GB[2 * mh + dh][:, t * P:(t + 1) * P], x1[:, 4 * mh + t, dh * P:(dh + 1) * P], ident[:, :])
                        last.then_inc(s["x1T_ps"], 1)

                def phase_b(b, update, prepare):
                    n = b + 1
                    done = [0]

                    def score_tiles(count):
                        if not prepare:
                            return
                        for u in range(done[0], done[0] + count):
                            t, h = u // H, u % H
                            if u < 2:
                                pe.wait_ge(s["vals_sb"], 2 * u + 2)
                            if u == 0:
                                for k in range(2):
                                    pe.wait_ge(s[f"stack_moved{k}"], 16 * 24)
                                if update:
                                    pe.wait_ge(s["prob_made"], PAIRS)
                            if u >= 2:
                                pe.wait_ge(s["score_sb"], u - 1)
                            for mh in range(NH):
                                last = pe.matmul(SP[u % 2][:, mh * HALF:(mh + 1) * HALF],
                                                 qst[h // GH][0:KROWS, h % GH, t * P:(t + 1) * P],
                                                 kst[h // GH][0:KROWS, h % GH, mh * HALF:(mh + 1) * HALF],
                                                 start=True, stop=True)
                            last.then_inc(s["score_ps"], 1)
                        done[0] += count

                    if not update:
                        for i in range(8):
                            project(n, i)
                    if prepare:
                        for i in range(2):
                            values(n, i)
                    if update and not general:
                        pe.wait_ge(s["att_sb"], 4)
                        if prepare:
                            pe.wait_ge(s["proj_sb"], 8)
                        for i in range(4):
                            for t in range(2):
                                for c in range(DC):
                                    last = pe.matmul(GB[i][:, t * D:(t + 1) * D], hT[:, c, (2 * i + t) * P:(2 * i + t + 1) * P],
                                                     w0["o"][:, c, :], start=(c == 0), stop=(c == DC - 1))
                            last.then_inc(s["y_ps"], 1)
                    if prepare:
                        for i in range(2, 4):
                            values(n, i)
                    score_tiles(16)
                    if update and not general:
                        pe.wait_ge(s["y_sum"], 4)
                        for m in range(NT):
                            for k in range(NT):
                                last = pe.matmul(GB[0][:, 2 * m:2 * m + 2], edge[:, k, m * P:(m + 1) * P], ones[:, 0:2],
                                                 start=(k == 0), stop=(k == NT - 1))
                        last.then_inc(s["cnt_ps"], 1)
                    score_tiles(4)
                    if update and not general:
                        pe.wait_ge(s["recip_made"], 1)
                        for mh in range(NH):
                            for i in range(4):
                                last = pe.matmul(GB[mh][:, i * P:(i + 1) * P], counts[:, 4 * mh + i:4 * mh + i + 1].broadcast_to([P, P]),
                                                 ident[:, :], start=True, stop=True)
                            last.then_inc(s["recip_ps"], 1)
                    score_tiles(4)
                    if update and not general:
                        pe.wait_ge(s["x1c_made"], 2)
                        pe.wait_ge(s["x1b_made"], 2)
                    for mh in range(0 if general else NH):
                        cols = slice(mh * HALF, (mh + 1) * HALF)
                        if update and mh == 1:
                            pe.wait_ge(s["recip_sb"], 2)
                            turn_x1(0)
                        for dh in range(DC):
                            if update and mh == 1:
                                pe.wait_ge(s["agg_sb"], dh + 1)
                            for k in range(NT):
                                if update:
                                    for e, part in enumerate((x1a, x1b, x1c)):
                                        last = pe.matmul(GB[2 + dh][:, :], part[:, k, dh * P:(dh + 1) * P], edge[:, k, cols],
                                                         start=(k == 0 and e == 0), stop=(k == NT - 1 and e == 2))
                                if k % 2 == 1:
                                    score_tiles(1)
                            if update:
                                last.then_inc(s["agg_ps"], 1)
                    for mh in range(NH):
                        if update and mh == 0 and general:
                            pe.wait_ge(s["recip_made"], 2 * labels)
                            turn_x1(0)
                        if update and mh == 1:
                            pe.wait_ge(s["s_made"], 2)
                            turn_x1(1)
                        score_tiles(1)
                        if update and mh == 0:
                            pe.wait_ge(s["agg_sb"], 4 * labels)
                        if mh == 1:
                            if update:
                                pe.wait_ge(s["new_made"], 2)
                                finish(before, (0, 1))
                            score_tiles(1)
                        for oh in range(DC):
                            if update and not general:
                                if mh == 1:
                                    pe.wait_ge(s["x1T_sb"], 3 + oh)
                                for c in range(DC):
                                    last = pe.matmul(GB[2 + oh][:, :], wd[:, c, oh * P:(oh + 1) * P],
                                                     aggT[:, c, mh * HALF:(mh + 1) * HALF], start=(c == 0), stop=(c == DC - 1))
                                last.then_inc(s["wd_ps"], 1)
                            score_tiles(int(mh + oh < 2))
                        for oh in range(DC):
                            q = 2 * mh + oh
                            o = slice(oh * P, (oh + 1) * P)
                            tiles = int(q < 3)

                            def products(bank, w, v, first, last):
                                if update:
                                    for c in range(DC):
                                        mm = pe.matmul(GB[bank][:, :], w1[w][:, c, o], v[:, c, :], start=(first and c == 0),
                                                       stop=(last and c == DC - 1))
                                    return mm

                            if update:
                                if oh == 0:
                                    pe.wait_ge(s["x1T_sb"], 2 * (mh + 1))
                                    if mh == 1:
                                        pe.wait_ge(s["fin_normed"], 4 * (before + 1))
                                if q > 0:
                                    pe.wait_ge(s["rt_made"], q)
                            products(0, "rh", x1T, True, False)
                            score_tiles(tiles)
                            if update:
                                pe.wait_ge(s["out_sb"], 2 * (mh + 1))
                                if q > 0:
                                    pe.wait_ge(s["t_made"], q)
                                products(3, "nh", x1T, True, True).then_inc(s["nh_ps"], 1)
                            score_tiles(tiles)
                            if update:
                                products(0, "ri", outT, False, True).then_inc(s["r_ps"], 1)
                            score_tiles(tiles)
                            if update:
                                if q > 0:
                                    pe.wait_ge(s["s_made"], q)
                                products(2, "ni", outT, True, True).then_inc(s["ni_ps"], 1)
                            score_tiles(tiles)
                            if update and q > 0:
                                pe.wait_ge(s["zt_made"], q)
                            products(1, "zh", x1T, True, False)
                            score_tiles(tiles)
                            if q == 2:
                                score_tiles(1)
                            if update:
                                products(1, "zi", outT, False, True).then_inc(s["z_ps"], 1)
                            if mh == 0:
                                score_tiles(1)
                            if q == 2 and prepare:
                                pe.wait_ge(s["shift_rounded"], 1)
                                pe.transpose(SP[0][0:H * NT, 0:P], shift_r[:, :, :].bitcast(F32).rearrange("p h t -> p (h t)"),
                                             ident[:, :]).then_inc(s["shift_ps"], 1)
                        if mh == 1 and after:
                            pe.wait_ge(s["new_made"], 4)
                            finish(before + 1, (0, 1))

                def label_sums():
                    pe.wait_ge(s["x1_in"], 16)
                    pe.wait_ge(s["ones_made"], 1)
                    pe.wait_ge(s["wd_in"], 16)
                    for mh in range(NH):
                        for d in range(LABELS):
                            r = LABELS * mh + d
                            pe.wait_ge(s["mask_made"], 2 * (r + 1))
                            if r > 0:
                                pe.wait_ge(s["cnt_sum"], r)
                            for k in range(NT):
                                last = pe.matmul(GB[0][:, :], ones_f, label_mask[:, k, :], start=(k == 0), stop=(k == NT - 1))
                            last.then_inc(s["cnt_ps"], 1)
                            if r > 0:
                                pe.wait_ge(s["agg_sb"], DC * r)
                            for dh in range(DC):
                                for k in range(NT):
                                    last = pe.matmul(GB[2 + dh][:, :], x1[:, k, dh * P:(dh + 1) * P], label_mask[:, k, :],
                                                     start=(k == 0), stop=(k == NT - 1))
                                last.then_inc(s["agg_ps"], 1)
                            pe.wait_ge(s["agg_sb"], DC * (r + 1))
                            for oh in range(DC):
                                for c in range(DC):
                                    last = pe.matmul(SP[mh][:, oh * HALF:(oh + 1) * HALF], label_wd[:, DC * d + c, oh * P:(oh + 1) * P],
                                                     aggT[:, c, mh * HALF:(mh + 1) * HALF], start=(d == 0 and c == 0),
                                                     stop=(d == LABELS - 1 and c == DC - 1))
                                if d == LABELS - 1:
                                    last.then_inc(s["wd_ps"], 1)
                                elif oh == DC - 1:
                                    last.then_inc(s["wd_part"], 1)

                if general:
                    label_sums()
                elif update:
                    phase_a(b, prepare)
                phase_b(b, update, prepare)

            @block.scalar
            def _(act):
                def project(n, i):
                    g, k, nh = i // 4, i // 2 % 2, i % 2
                    act.wait_ge(s["proj_ps"], i + 1)
                    if g == 1 and nh == 0:
                        act.wait_ge(s[f"stack_moved{k}"], 16 * 12)
                    act.activation(lows[k][:, nh * HALF:(nh + 1) * HALF], GB[2][:, :], ACT.Identity, bias=col[("bq", "bk")[k]][:, g:g + 1],
                                   scale=(SCALE, 1.0)[k]).then_inc(s["proj_sb"], 1)

                def phase_a(b, more_to_come):
                    for j in range(QUARTERS):
                        for t in range(NT):
                            q = j * NT + t
                            if q >= PSLOTS:
                                act.wait_ge(s["pv_done"], q - PSLOTS + 1)
                            for hp in range(2):
                                p = 2 * q + hp
                                act.wait_ge(s["st_ps"], p + 1)
                                act.activation(probs[q % PSLOTS][:, 2 * hp:2 * hp + 2, :],
                                               SP[p % 2][:, :].rearrange("p (h n) -> p h n", h=2), ACT.Exp).then_inc(s["prob_made"], 1)
                            if t == 5:
                                act.wait_ge(s["rec_ps"], j + 1)
                                if j > 0:
                                    act.wait_ge(s["att_sb"], j)
                                act.activation(recb[:, :], GB[3][:, :], ACT.Copy).then_inc(s["rec_sb"], 1)
                            if more_to_come and q >= 2 * NT + 2 and t % 2 == 0:
                                project(b + 1, (q - 2 * NT) // 2 - 1)
                    if more_to_come:
                        project(b + 1, 7)

                def phase_b(b, update, prepare):
                    n = b + 1
                    done = [0]

                    def score_tiles(count):
                        if not prepare:
                            return
                        for u in range(done[0], done[0] + count):
                            t, h = u // H, u % H
                            act.wait_ge(s["score_sb"], u + 1)
                            act.activation(scores[u % SLOTS][:, :], scores[u % SLOTS][:, :], ACT.Exp, scale=-1.0,
                                           bias=negmax[:, h, t:t + 1], accum_out=rowsum[:, h, t:t + 1]).then_inc(s["exp_made"], 1)
                        done[0] += count

                    def x1T_in(mh):
                        for dh in range(DC):
                            act.wait_ge(s["x1T_ps"], 2 * mh + dh + 1)
                            if mh == 1:
                                act.wait_ge(s["new_made"], 2)
                            act.activation(x1T[:, dh, :], GB[2 * mh + dh][:, :], ACT.Copy).then_inc(s["x1T_sb"], 1)

                    def look_through(i):
                        if prepare:
                            act.wait_ge(s["edge_made"], i + 1)
                            act.activation(adj_t[i % 4], adj_t[i % 4], ACT.Square, bias=minus_half[:, :], accum_out=more[:, i:i + 1]).then_inc(s["more_read"], 1)

                    if not update:
                        for i in range(8):
                            project(n, i)
                    score_tiles(14)
                    if update and not general:
                        for e in range(2):
                            half = slice(4 * e, 4 * e + 4)
                            act.wait_ge(s["x1_made"], e + 1)
                            act.wait_ge(s["att_sb"], 4)
                            act.wait_ge(s["y_ps"], 4)
                            act.activation(x1a[:, half, :], x1[:, half, :], ACT.Copy).then_inc(s["x1a_made"], 1)
                    score_tiles(5)
                    if update and not general:
                        for e in range(2):
                            half = slice(4 * e, 4 * e + 4)
                            act.wait_ge(s["rest_made"], e + 1)
                            act.activation(x1b[:, half, :], rest[:, half, :], ACT.Copy).then_inc(s["x1b_made"], 1)
                    score_tiles(5)
                    if update and not general:
                        for mh in range(NH):
                            act.wait_ge(s["recip_ps"], mh + 1)
                            act.activation(recip[:, mh * HALF:(mh + 1) * HALF], GB[mh][:, :], ACT.Copy).then_inc(s["recip_sb"], 1)
                    score_tiles(12)
                    if update and not general:
                        x1T_in(0)
                    score_tiles(4)
                    for mh in range(NH):
                        if update and (mh == 1 or general):
                            x1T_in(mh)
                        score_tiles(1 + mh)
                        for oh in range(DC):
                            if update:
                                act.wait_ge(s["wd_ps"], 2 * mh + oh + 1)
                                product = SP[mh][:, oh * HALF:(oh + 1) * HALF] if general else GB[2 + oh][:, :]
                                act.activation(outT[:, oh, :], product, ACT.Relu, bias=col["bd"][:, oh:oh + 1]).then_inc(s["out_sb"], 1)
                            if mh == 0 and oh == 0:
                                score_tiles(1)
                        score_tiles(1)
                        if mh == 0:
                            for i in range(3):
                                look_through(i)
                        for oh in range(DC):
                            q = 2 * mh + oh
                            tiles = int(q < 3)
                            score_tiles(2 * tiles)
                            if update:
                                act.wait_ge(s["r_ps"], q + 1)
                                if q == 0 and not general:
                                    act.wait_ge(s["x1c_made"], 2)
                                act.activation(rT[:, oh, :], GB[0][:, :], ACT.Tanh, bias=col["bri"][:, oh:oh + 1], scale=0.5).then_inc(s["rt_made"], 1)
                            score_tiles(tiles)
                            if mh == 0:
                                look_through(3 + 2 * oh)
                            score_tiles(tiles)
                            if update:
                                act.wait_ge(s["s_made"], q + 1)
                                act.activation(nT[:, oh, :], nT[:, oh, :], ACT.Tanh, bias=col["bni"][:, oh:oh + 1]).then_inc(s["n_made"], 1)
                            score_tiles(tiles)
                            if mh == 0:
                                look_through(4 + 2 * oh)
                            if q == 2:
                                score_tiles(1)
                            if update:
                                act.wait_ge(s["z_ps"], q + 1)
                                act.activation(zT[:, oh, :], GB[1][:, :], ACT.Tanh, bias=col["bzi"][:, oh:oh + 1], scale=0.5).then_inc(s["zt_made"], 1)
                            if mh == 0:
                                score_tiles(1)
                            if q == 1:
                                look_through(7)
                            if q == 2 and prepare:
                                act.wait_ge(s["excess_made"], 1)
                                act.activation(excess[:, :, :], excess[:, :, :], ACT.Exp).then_inc(s["excess_exp"], 1)

                if update and not general:
                    phase_a(b, prepare)
                phase_b(b, update, prepare)

            @block.vector
            def _(dve):
                def high_part(n, i):
                    g, k, nh = i // 4, i // 2 % 2, i % 2
                    cols = slice(nh * HALF, (nh + 1) * HALF)
                    dve.wait_ge(s["proj_sb"], i + 1)
                    dve.tensor_copy(highs_r[k][:, cols], lows[k][:, cols]).then_inc(s["hi_made"], 1)

                def finish_stats(f, banks):
                    for k, bank in enumerate(banks):
                        dve.wait_ge(s["fin_ps"], 2 * f + k + 1)
                        if f + k > 0:
                            dve.wait_ge(s["mv2_made"], 4 * f + 2 * k)
                        for t in range(2):
                            dve.bn_stats(stats2[:, t, :], GB[bank][:, t * D:(t + 1) * D]).then_inc(s["st2_made"], 1)
                        for t in range(2):
                            dve.wait_ge(s["st2_made"], 4 * f + 2 * k + t + 1)
                            dve.bn_aggr(mv2[:, 2 * k + t, :], stats2[:, t, :]).then_inc(s["mv2_made"], 1)

                def finish_norm(f, banks):
                    dve.wait_ge(s["rstd2_made"], f + 1)
                    if f > 0:
                        dve.wait_ge(s["fin_saved"], 16 * f)
                    for t in range(4):
                        dve.tensor_scalar(final[:, t, :], GB[banks[t // 2]][:, t % 2 * D:(t % 2 + 1) * D], mv2[:, t, 0:1],
                                          rstd2[:, t:t + 1], ALU.subtract, ALU.mult).then_inc(s["fin_normed"], 1)

                def phase_a(b, more_to_come):
                    def normalise(j):
                        g, nh = j // NH, j % NH
                        dve.wait_ge(s["pv_done"], NT * (j + 1))
                        dve.wait_ge(s["rec_sb"], j + 1)
                        dve.tensor_tensor(hT[:, g, nh * HALF:(nh + 1) * HALF], GB[j % 2][:, :], recb[:, :], ALU.mult).then_inc(s["att_sb"], 1)

                    for j in range(QUARTERS):
                        for t in range(NT):
                            for hp in range(2):
                                p = (j * NT + t) * 2 + hp
                                dve.wait_ge(s["prob_made"], p + 1)
                                tile = probs[(j * NT + t) % PSLOTS][:, 2 * hp:2 * hp + 2, :]
                                dve.tensor_tensor(tile, tile, bc(edge[:, t, j % NH * HALF:(j % NH + 1) * HALF], [P, 2, HALF]),
                                                  ALU.min).then_inc(s["prob_masked"], 1)
                            if j > 0 and t == 3:
                                normalise(j - 1)
                            if before and j == 0 and t == 6:
                                finish_stats(0, (1, 2))
                            if before and j == 0 and t == 7:
                                finish_norm(0, (1, 2))
                            if more_to_come and j * NT + t >= 2 * NT + 3 and t % 2 == 1:
                                high_part(b + 1, (j * NT + t - 2 * NT - 3) // 2)
                    if more_to_come:
                        high_part(b + 1, 7)
                    normalise(QUARTERS - 1)

                def phase_b(b, update, prepare):
                    n = b + 1
                    done = [0]

                    def score_tiles(count):
                        if not prepare:
                            return
                        for u in range(done[0], done[0] + count):
                            t, h = u // H, u % H
                            if h == 0:
                                dve.wait_ge(s[f"adjn_in{t % 2}"], 16 * (t // 2 + 1))
                                if u > H:
                                    dve.wait_ge(s["score_sb"], u - H)
                                dve.tensor_scalar(bias[t % 2][:, :], adj_n[t % 2][:, :], 0.0, NOEDGE,
                                                  ALU.is_equal, ALU.mult).then_inc(s["bias_made"], 1)
                                dve.wait_ge(s["bias_made"], t + 1)
                            dve.wait_ge(s["score_ps"], u + 1)
                            if u >= SLOTS:
                                dve.wait_ge(s["exp_made"], u - SLOTS + 1)
                            dve.tensor_tensor_reduce(out=scores[u % SLOTS][:, :], in0=SP[u % 2][:, :], in1=bias[t % 2][:, :],
                                                     scale=-1.0, scalar=-NEG_INF, op0=ALU.add, op1=ALU.min,
                                                     accum_out=negmax[:, h, t:t + 1]).then_inc(s["score_sb"], 1)
                        done[0] += count

                    def values(first, end):
                        for i in range(first, end):
                            dve.wait_ge(s["vals_ps"], i + 1)
                            dve.tensor_tensor(vals[:, 2 * i:2 * i + 2, :], SP[i // 2][:, i % 2 * HALF:(i % 2 + 1) * HALF].rearrange("p (t d) -> p t d", t=2),
                                              bc(row["bv"][:, :], [P, 2, D]), ALU.add).then_inc(s["vals_sb"], 1)

                    def combine(q):
                        oh = q % 2
                        dve.wait_ge(s["n_made"], q + 1)
                        dve.tensor_tensor(rT[:, oh, :], x1T[:, oh, :], nT[:, oh, :], ALU.subtract).then_inc(s["diff_made"], 1)
                        dve.wait_ge(s["diff_made"], q + 1)
                        dve.wait_ge(s["zt_made"], q + 1)
                        dve.scalar_tensor_tensor(rT[:, oh, :], zT[:, oh, :], 1.0, rT[:, oh, :], ALU.add, ALU.mult).then_inc(s["prod_made"], 1)
                        dve.wait_ge(s["prod_made"], q + 1)
                        dve.scalar_tensor_tensor(nT[:, oh, :], rT[:, oh, :], 0.5, nT[:, oh, :], ALU.mult, ALU.add).then_inc(s["new_made"], 1)

                    def edges(i):
                        if prepare:
                            dve.wait_ge(s[f"adjt_in{i % 4}"], 16 * (i // 4 + 1))
                            if i == 0:
                                if update:
                                    dve.wait_ge(s["agg_ps"], 4)
                                if update:
                                    dve.wait_ge(s["cnt_ps"], 1)
                            dve.tensor_scalar(edge[:, i, :], adj_t[i % 4], 0.0, EDGE, ALU.not_equal, ALU.mult).then_inc(s["edge_made"], 1)

                    if not update:
                        for i in range(8):
                            high_part(n, i)
                    if prepare:
                        values(0, 2)
                    if update and not general:
                        dve.wait_ge(s["biased"], 1)
                        for i in range(4):
                            two = slice(2 * i, 2 * i + 2)
                            dve.wait_ge(s["y_ps"], i + 1)
                            dve.tensor_tensor(x1[:, two, :], GB[i][:, :].rearrange("p (t d) -> p t d", t=2), x1[:, two, :],
                                              ALU.add).then_inc(s["y_sum"], 1)
                            dve.wait_ge(s["y_sum"], i + 1)
                            if i > 0:
                                dve.wait_ge(s["mv_made"], 2 * i)
                            for t in range(2):
                                dve.bn_stats(stats[:, t, :], x1[:, 2 * i + t, :]).then_inc(s["stats_made"], 1)
                            for t in range(2):
                                dve.wait_ge(s["stats_made"], 2 * i + t + 1)
                                dve.bn_aggr(mv[:, 2 * i + t, :], stats[:, t, :]).then_inc(s["mv_made"], 1)
                    if prepare:
                        values(2, 4)
                    score_tiles(4)
                    if update and not general:
                        dve.wait_ge(s["rstd_made"], 1)
                        for t in range(NT):
                            dve.tensor_scalar(x1[:, t, :], x1[:, t, :], mv[:, t, 0:1], rstd[:, t:t + 1],
                                              ALU.subtract, ALU.mult).then_inc(s["normed"], 1)
                    score_tiles(14)
                    if update and not general:
                        dve.wait_ge(s["cnt_ps"], 1)
                        dve.tensor_scalar(counts[:, :], GB[0][:, 0:2 * NT:2], EDGE * EPS_COUNT, None, ALU.add).then_inc(s["cnt_sum"], 1)
                        dve.wait_ge(s["cnt_sum"], 1)
                        dve.reciprocal(counts[:, :], counts[:, :]).then_inc(s["recip_made"], 1)
                    score_tiles(6)
                    for mh in range(0 if general else NH):
                        for dh in range(DC):
                            score_tiles(4)
                            if update:
                                dve.wait_ge(s["agg_ps"], 2 * mh + dh + 1)
                                dve.wait_ge(s["recip_sb"], mh + 1)
                                dve.tensor_tensor(aggT[:, dh, mh * HALF:(mh + 1) * HALF], GB[2 + dh][:, :],
                                                  recip[:, mh * HALF:(mh + 1) * HALF],
                                                  ALU.mult).then_inc(s["agg_sb"], 1)
                    for mh in range(NH):
                        score_tiles(1)
                        if mh == 0:
                            edges(0)
                            for oh in range(DC):
                                score_tiles(1)
                                edges(1 + oh)
                        else:
                            if update:
                                finish_stats(before, (0, 1))
                            score_tiles(1)
                            if update:
                                finish_norm(before, (0, 1))
                            score_tiles(1)
                        for oh in range(DC):
                            q = 2 * mh + oh
                            tiles = int(q < 3)
                            score_tiles(2 * tiles)
                            if update and oh == 1:
                                combine(q - 1)
                            score_tiles(tiles)
                            if update:
                                dve.wait_ge(s["rt_made"], q + 1)
                                dve.tensor_scalar(rT[:, oh, :], rT[:, oh, :], 0.5, 0.5, ALU.mult, ALU.add).then_inc(s["r_made"], 1)
                                dve.wait_ge(s["r_made"], q + 1)
                                dve.wait_ge(s["nh_ps"], q + 1)
                                dve.scalar_tensor_tensor(nT[:, oh, :], GB[3][:, :], col["bnh"][:, oh:oh + 1], rT[:, oh, :],
                                                         ALU.add, ALU.mult).then_inc(s["t_made"], 1)
                            if mh == 0:
                                edges(3 + 2 * oh)
                            score_tiles(tiles)
                            if update:
                                dve.wait_ge(s["ni_ps"], q + 1)
                                dve.wait_ge(s["t_made"], q + 1)
                                dve.tensor_tensor(nT[:, oh, :], GB[2][:, :], nT[:, oh, :], ALU.add).then_inc(s["s_made"], 1)
                            if mh == 0:
                                edges(4 + 2 * oh)
                            score_tiles((1 + mh) * tiles)
                            if q == 2 and prepare:
                                dve.wait_ge(s["score_sb"], TILES)
                                dve.tensor_copy(shift_r[:, :, :], negmax[:, :, :]).then_inc(s["shift_rounded"], 1)
                                dve.wait_ge(s["shift_rounded"], 1)
                                dve.tensor_tensor(excess[:, :, :], shift_r[:, :, :].bitcast(F32), negmax[:, :, :],
                                                  ALU.subtract).then_inc(s["excess_made"], 1)
                            if mh == 0:
                                score_tiles(1)
                            if q == 1:
                                edges(7)
                            if q == 2 and prepare:
                                dve.wait_ge(s["shift_ps"], 1)
                                dve.tensor_copy(shift[:, :], SP[0][0:H * NT, 0:P]).then_inc(s["shift_sb"], 1)
                        if update:
                            combine(2 * mh + 1)
                        if mh == 1 and prepare:
                            dve.wait_ge(s["exp_made"], TILES)
                            dve.wait_ge(s["excess_exp"], 1)
                            dve.tensor_tensor(rowsum[:, :, :], rowsum[:, :, :], excess[:, :, :], ALU.mult).then_inc(s["sum_shifted"], 1)
                            dve.wait_ge(s["sum_shifted"], 1)
                            if update:
                                dve.wait_ge(s["rec_ps"], 4)
                            dve.reciprocal(recsum[:, :, :], rowsum[:, :, :]).then_inc(s["recsum_made"], 1)
                            dve.wait_ge(s["more_read"], NT)
                            dve.tensor_tensor(more_any[:, :], more_any[:, :], more[:, :], ALU.add).then_inc(s["more_made"], 1)
                        if mh == 1 and after:
                            finish_stats(before + 1, (0, 1))
                            finish_norm(before + 1, (0, 1))

                def label_masks():
                    dve.memset(ones_f, 1.0).then_inc(s["ones_made"], 1)
                    for mh in range(NH):
                        for d in range(LABELS):
                            r = LABELS * mh + d
                            dve.wait_ge(s["labels_in"], 32 * (mh + 1))
                            if r > 0:
                                dve.wait_ge(s["agg_ps"], DC * r)
                            if r > 0:
                                dve.wait_ge(s["cnt_ps"], r)
                            for e in range(2):
                                dve.tensor_scalar(label_mask[:, e * NT // 2:(e + 1) * NT // 2, :], label_adj[e], float(d + 1), None,
                                                  ALU.is_equal).then_inc(s["mask_made"], 1)
                            dve.wait_ge(s["cnt_ps"], r + 1)
                            if r > 0:
                                dve.wait_ge(s["agg_sb"], DC * r)
                            dve.tensor_scalar(recip[:, 0:HALF], GB[0][:, :], EPS_COUNT, None, ALU.add).then_inc(s["cnt_sum"], 1)
                            dve.wait_ge(s["cnt_sum"], r + 1)
                            dve.reciprocal(recip[:, 0:HALF], recip[:, 0:HALF]).then_inc(s["recip_made"], 1)
                            dve.wait_ge(s["recip_made"], r + 1)
                            if d > 0:
                                dve.wait_ge(s["wd_part"], (LABELS - 1) * mh + d)
                            for dh in range(DC):
                                dve.wait_ge(s["agg_ps"], DC * r + dh + 1)
                                dve.tensor_tensor(aggT[:, dh, mh * HALF:(mh + 1) * HALF], GB[2 + dh][:, :], recip[:, 0:HALF],
                                                  ALU.mult).then_inc(s["agg_sb"], 1)

                if general:
                    label_masks()
                elif update:
                    phase_a(b, prepare)
                phase_b(b, update, prepare)

            @block.gpsimd
            def _(pool):
                def low_part(n, i):
                    g, k, nh = i // 4, i // 2 % 2, i % 2
                    cols = slice(nh * HALF, (nh + 1) * HALF)
                    pool.wait_ge(s["hi_made"], i + 1)
                    pool.tensor_tensor(lows_r[k][:, cols], lows[k][:, cols], highs_r[k][:, cols].bitcast(F32),
                                       ALU.subtract).then_inc(s["lo_made"], 1)

                def finish(f, b, mh):
                    pool.wait_ge(s["mv2_made"], 4 * (f + 1))
                    pool.tensor_scalar(small2[:, :], mv2[:, :, 1], EPS0, None, ALU.add).then_inc(s["eps2_added"], 1)
                    pool.wait_ge(s["eps2_added"], f + 1)
                    pool.tensor_tensor(rstd2[:, :], small2[:, :], half_power[:, 0:4], ALU.pow).then_inc(s["rstd2_made"], 1)
                    pool.wait_ge(s["fin_normed"], 4 * (f + 1))
                    pool.tensor_tensor(final[:, :, :], final[:, :, :], bc(row["g1"][:, :], [P, 4, D]), ALU.mult).then_inc(s["fin_scaled"], 1)
                    pool.wait_ge(s["fin_scaled"], f + 1)
                    pool.tensor_tensor(final[:, :, :], final[:, :, :], bc(row["b1"][:, :], [P, 4, D]), ALU.add).then_inc(s["fin_made"], 1)
                    pool.wait_ge(s["fin_made"], f + 1)
                    pool.dma_start(out[b, mh * HALF:(mh + 1) * HALF, :].rearrange("(t p) d -> p t d", p=P),
                                   final[:, :, :]).then_inc(s["fin_saved"], 16)

                def phase_a(b, more_to_come):
                    pool.wait_ge(s["x1_in"], 16)
                    pool.tensor_tensor(x1[:, :, :], x1[:, :, :], bc(row["bo"][:, :], [P, NT, D]), ALU.add).then_inc(s["biased"], 1)
                    if before:
                        finish(0, b - 1, 1)
                    if more_to_come:
                        for i in range(8):
                            low_part(b + 1, i)

                def attend(b):
                    pool.wait_ge(s["mv_made"], NT)
                    pool.tensor_scalar(small[:, :], mv[:, :, 1], EPS0, None, ALU.add).then_inc(s["eps_added"], 1)
                    pool.wait_ge(s["eps_added"], 1)
                    pool.tensor_tensor(rstd[:, :], small[:, :], half_power[:, :], ALU.pow).then_inc(s["rstd_made"], 1)
                    for e in range(2):
                        half = slice(4 * e, 4 * e + 4)
                        pool.wait_ge(s["normed"], 4 * (e + 1))
                        pool.tensor_tensor(x1[:, half, :], x1[:, half, :], bc(row["g0"][:, :], [P, 4, D]), ALU.mult).then_inc(s["scaled"], 1)
                        pool.wait_ge(s["scaled"], e + 1)
                        pool.tensor_tensor(x1[:, half, :], x1[:, half, :], bc(row["b0"][:, :], [P, 4, D]), ALU.add).then_inc(s["x1_made"], 1)
                    pool.wait_ge(s["x1_made"], 2)
                    pool.dma_start(x1_dram[b].rearrange("(t p) d -> p t d", p=P), x1[:, :, :]).then_inc(s["x1_saved"], 16)
                    for e in range(2):
                        half = slice(4 * e, 4 * e + 4)
                        pool.wait_ge(s["x1a_made"], e + 1)
                        pool.wait_ge(s["pv_done"], QUARTERS * NT)
                        pool.tensor_tensor(rest[:, half, :], x1[:, half, :], x1a[:, half, :], ALU.subtract).then_inc(s["rest_made"], 1)
                    for e in range(2):
                        half = slice(4 * e, 4 * e + 4)
                        pool.wait_ge(s["x1b_made"], e + 1)
                        if prepare:
                            for k in range(2):
                                pool.wait_ge(s[f"stack_moved{k}"], 16 * 24)
                        pool.tensor_tensor(x1c[:, half, :], rest[:, half, :], x1b[:, half, :], ALU.subtract).then_inc(s["x1c_made"], 1)

                def phase_b(b, update, prepare):
                    n = b + 1
                    if not update:
                        for i in range(8):
                            low_part(n, i)
                    if not update:
                        return
                    if not general:
                        attend(b)
                    for mh in range(NH):
                        if mh == 0 or after:
                            finish(before + mh, b, mh)

                if update and not general:
                    phase_a(b, prepare)
                phase_b(b, update, prepare)
                if update:
                    pool.wait_ge(s["fin_saved"], 16 * (before + 1 + after))
                if update and not general:
                    pool.wait_ge(s["x1_saved"], 16)


            ctx_step.close()
            nc.clear_and_free_semaphores(list(s.values()))
            nc.all_engine_barrier()

        step(-1, 0, 1)
        step(0, 1, 1)
        with nc.Fori(1, B - 1) as b:
            step(b, 1, 1, before=1)
        step(B - 1, 1, 0, before=1, after=1)

        flag_made, flag_ps, flag_sb, flag_read = (nc.alloc_semaphore(n) for n in ("flag_made", "flag_ps", "flag_sb", "flag_read"))
        with nc.Block() as block:
            @block.vector
            def _(dve):
                dve.tensor_reduce(flag[:, :], more_any[:, :], AX.X, ALU.max).then_inc(flag_made, 1)
                dve.wait_ge(flag_made, 1)
                dve.tensor_scalar(flags[:, :], flag[:, :].broadcast_to([P, 2]), 0.0, None, ALU.is_gt).then_inc(flag_made, 1)
                dve.wait_ge(flag_ps, 1)
                dve.tensor_scalar(general_flag[:, :], SP[0][0:1, 0:1], 0.0, None, ALU.is_gt).then_inc(flag_sb, 1)

            @block.tensor
            def _(pe):
                pe.wait_ge(flag_made, 2)
                pe.matmul(SP[0][:, 0:2], ones[:, :], flags[:, :], start=True, stop=True).then_inc(flag_ps, 1)

        nc.clear_and_free_semaphores([flag_made, flag_ps, flag_sb, flag_read])
        nc.all_engine_barrier()
        general = nc.values_load(general_flag[0:1, 0:1], min_val=0, max_val=1)
        with nc.If(general > 0):
            with nc.Fori(0, B) as b:
                step(b, 1, 0, after=1, general=1)


_NAMES = {"Wq": "L0_gnn_Wq", "Wk": "L0_gnn_Wk", "Wv": "L0_gnn_Wv", "Wo": "L0_gnn_Wo",
          "bv": "L0_gnn_bv", "bo": "L0_gnn_bo",
          "g0": "L0_gnn_gamma", "b0": "L0_gnn_beta", "g1": "L1_gnn_gamma", "b1": "L1_gnn_beta"}
_COLUMNS = ("L0_gnn_bq", "L0_gnn_bk", "L1_gnn_bd", "L1_gnn_bri", "L1_gnn_brh", "L1_gnn_bzi",
            "L1_gnn_bzh", "L1_gnn_bni", "L1_gnn_bnh")
_TURNED = {"Wd": "L1_gnn_Wd", "Wri": "L1_gnn_Wri", "Wrh": "L1_gnn_Wrh", "Wzi": "L1_gnn_Wzi",
           "Wzh": "L1_gnn_Wzh", "Wni": "L1_gnn_Wni", "Wnh": "L1_gnn_Wnh"}


def kernel(**inputs):
    import numpy as _np
    import concourse.bacc as _bacc
    from concourse import mybir as _mybir
    from concourse.bass_utils import run_bass_kernel_spmd as _run

    laid = {"x": _np.ascontiguousarray(inputs["x"]), "adj": _np.ascontiguousarray(inputs["adj"]),
            "xT": _np.ascontiguousarray(_np.asarray(inputs["x"]).transpose(0, 2, 1)),
            "adjT": _np.ascontiguousarray(_np.asarray(inputs["adj"]).transpose(0, 2, 1))}
    for k, v in _NAMES.items():
        laid[k] = _np.ascontiguousarray(inputs[v])
    for k, v in _TURNED.items():
        laid[k] = _np.ascontiguousarray(_np.asarray(inputs[v]).T)
    columns = _np.stack([_np.asarray(inputs[v]).reshape(DC, P) for v in _COLUMNS])
    laid["columns"] = _np.ascontiguousarray(columns.transpose(2, 0, 1))

    nc = _bacc.Bacc("TRN2", target_bir_lowering=False, num_devices=1)
    aps = {k: nc.dram_tensor(f"in_{k}", v.shape, _mybir.dt.from_np(v.dtype), kind="ExternalInput").ap()
           for k, v in laid.items()}
    out = nc.dram_tensor("out", (B, N, D), _mybir.dt.float32, kind="ExternalOutput").ap()
    graph_kernel(nc, aps, out)
    r = _run(nc, [{f"in_{k}": v for k, v in laid.items()}], core_ids=[0])
    return r.results[0]["out"]
```

```python
from contextlib import ExitStack

import numpy as np

import concourse.bass as bass
from concourse import mybir

F32 = mybir.dt.float32
F32R = mybir.dt.float32r
BF16 = mybir.dt.bfloat16
I32 = mybir.dt.int32
ALU = mybir.AluOpType
ACT = mybir.ActivationFunctionType
AX = mybir.AxisListType

P = 128
B, N, D, H = 8, 1024, 256, 8
HD = D // H
DC = D // P
NT = N // P
HALF = 512
NH = N // HALF
QUARTERS = 4
LAG = 2
GH = P // HD
G = H // GH
LABELS = 4
KROWS = 3 * HD
SROW = KROWS
SCALE = float(np.float32(1.0) / np.sqrt(HD).astype(np.float32))
EDGE = 2.0 ** 60
NOEDGE = -1.0e30
EPS0 = 1e-5
EPS_COUNT = 1e-8
NEG_INF = -3.0e38
SLOTS = 2
R_BANK, NI_BANK = (0, 2), (2, 0)
ACT_X1A = 7
PROJECT_AT = (8, 10, 12, 14, 21, 23, 25, 27)
PSLOTS = 3
TILES = NT * H
COLUMNS = ("bv", "bq", "bk", "bd", "bri", "brh", "bzi", "bzh", "bni", "bnh")
ALL_01 = N // 4
N_CONST = 17
PAIRS = QUARTERS * NT * 2


def graph_kernel(nc, a, out):
    ctx = ExitStack()
    with ctx:
        def sb(name, shape, dt):
            return ctx.enter_context(nc.sbuf_tensor(name, shape, dt))

        x1_dram = nc.dram_tensor("x1_scratch", (B, N, D), F32, kind="Internal").ap()

        shift_dram = nc.dram_tensor("shift_scratch", (H * NT, P), F32, kind="Internal").ap()

        w0 = {k: sb(f"w_{k}", [P, DC, D], F32) for k in ("q", "k", "v", "o")}
        w1 = {k: sb(f"w_{k}", [P, DC, D], F32) for k in ("ri", "rh", "zi", "zh", "ni", "nh")}
        wd = sb("wd", [P, DC, D], F32)
        cols = sb("cols", [P, len(COLUMNS), DC], F32)
        col = {k: cols[:, i, :] for i, k in enumerate(COLUMNS)}
        row = {k: sb(f"row_{k}", [P, D], F32) for k in ("bo", "g0", "b0", "g1", "b1")}
        ident = sb("ident", [P, P], F32)
        ones = sb("ones", [P, P], BF16)
        half_power = sb("half_power", [P, NT], F32)

        xT = sb("xT", [P, DC, N], F32)
        x1 = sb("x1", [P, NT, D], F32)
        kst = [sb(f"kst{g}", [P, GH, N], F32R) for g in range(G)]
        qst = [sb(f"qst{g}", [P, GH, N], F32R) for g in range(G)]
        vals = sb("vals", [P, NT, D], F32)
        edge = sb("edge", [P, NT, N], BF16)
        bias = [sb(f"bias{i}", [P, N], BF16) for i in range(2)]
        adj_n = [sb(f"adj_n{i}", [P, N], I32) for i in range(2)]
        adj_t0 = sb("adj_t", [P, N], I32)
        scores = [sb(f"scores{i}", [P, N], F32) for i in range(SLOTS)]
        recip = sb("recip", [P, N], F32)
        counts = sb("counts", [P, NT], F32)
        scores_r = [scores[i][:, :].bitcast(F32R) for i in range(2)]
        negmax = sb("negmax", [P, H, NT], F32)
        shift_r = sb("shift_r", [P, H, NT], F32R)
        excess = sb("excess", [P, H, NT], F32)
        rowsum = sb("rowsum", [P, H, NT], F32)
        recsum = sb("recsum", [P, H, NT], F32)
        shift = sb("shift", [H * NT, P], F32)
        recb = recip[:, 0:HALF]
        more = sb("more", [P, NT], F32)
        more_any = sb("more_any", [P, NT], F32)
        stats = sb("stats", [P, 2, 6], F32)
        mv = sb("mv", [P, NT, 2], F32)
        rstd = sb("rstd", [P, NT], F32)
        small = sb("small", [P, NT], F32)
        stats2 = sb("stats2", [P, 2, 6], F32)
        mv2 = sb("mv2", [P, 4, 2], F32)
        rstd2 = sb("rstd2", [P, 4], F32)
        small2 = sb("small2", [P, 4], F32)
        shift2 = sb("shift2", [P, 4], F32)
        minus_half = sb("minus_half", [P, 1], F32)
        flag = sb("flag", [P, 1], F32)
        flags = sb("flags", [P, 2], BF16)
        general_flag = sb("general_flag", [1, 1], I32)

        ground = sb("ground", [P, 14 * HALF], F32)
        probs = [ground[:, i * 2048:(i + 1) * 2048].rearrange("p (h n) -> p h n", h=GH)
                 for i in range(PSLOTS)]

        def area(i, n):
            return ground[:, i * HALF:(i + n) * HALF]

        x1T = area(0, 2).rearrange("p (c n) -> p c n", c=DC)
        aggT = area(2, 4).rearrange("p (c n) -> p c n", c=DC)
        x1Ts = [x1T, aggT[:, :, 0:HALF]]
        outT = area(6, 2).rearrange("p (c n) -> p c n", c=DC)
        rT = area(8, 2).rearrange("p (c n) -> p c n", c=DC)
        zT = area(10, 2).rearrange("p (c n) -> p c n", c=DC)
        nT = area(12, 2).rearrange("p (c n) -> p c n", c=DC)
        rest = area(8, 4).rearrange("p (t d) -> p t d", t=NT)
        turned = sb("turned", [P, DC * N], F32)
        hT = turned[:, :].rearrange("p (c n) -> p c n", c=DC)
        x1a = turned[:, 0:N].bitcast(BF16).rearrange("p (t d) -> p t d", t=NT)
        x1b = turned[:, N:2 * N].bitcast(BF16).rearrange("p (t d) -> p t d", t=NT)
        x1c = sb("x1c", [P, NT, D], BF16)
        final = sb("final", [P, 4, D], F32)

        def whole(buf, dt):
            return buf[:, :, :].bitcast(dt).rearrange("p a b -> p (a b)")

        lows = [scores[1][:, :], whole(x1c, F32)]
        lows_r = [scores_r[1], whole(x1c, F32R)]
        highs_r = [scores_r[0], adj_t0[:, :].bitcast(F32R)]

        adj_t = [adj_t0[:, :], whole(x1c, I32)] + [turned[:, e * N:(e + 1) * N].bitcast(I32) for e in range(2)]

        label_adj = [buf[:, :, :].bitcast(I32).rearrange("p a b -> p (a b)").rearrange("p (k n) -> p k n", k=NT // 2)
                     for buf in (xT, vals)]
        label_mask = edge[:, :, :].bitcast(F32)
        label_wd = turned[:, :].rearrange("p (k n) -> p k n", k=LABELS * DC)
        ones_f = w0["q"][:, 0, 0:P]

        SP = [ctx.enter_context(nc.psum_tensor(f"SP{i}", [P, N], F32)) for i in range(2)]
        GB = [ctx.enter_context(nc.psum_tensor(f"GB{i}", [P, HALF], F32)) for i in range(4)]

        names = """xT_in x1_in adjn_in0 adjn_in1 adjt_in0 adjt_in1 adjt_in2 adjt_in3
            proj_ps proj_sb hi_made lo_made stack_moved00 stack_moved01 stack_moved10 stack_moved11 vals_ps vals_sb bias_made edge_made more_read
            score_ps score_sb exp_made shift_ps shift_sb shift_moved recsum_made shift_rounded excess_made excess_exp sum_shifted
            st_ps prob_made prob_masked pv_done att_sb rec_ps rec_sb biased
            y_ps y_sum mv_made eps_added rstd_made normed scaled x1_made x1a_made rest_made x1b_made x1c_made x1_saved
            x1T_ps x1T_sb cnt_ps cnt_sum recip_made recip_ps recip_sb agg_ps agg_sb wd_ps out_sb
            r_ps z_ps ni_ps nh_ps rt_made zt_made nh_sb t_made s_made n_made diff_made prod_made new_made
            fin_ps st2_made mv2_made eps2_added rstd2_made scaled_mean2 shift2_made fin_normed fin_scaled fin_made fin_saved
            stats_made more_made shift_out
            wd_part wd_in labels_in ones_made mask_made""".split()

        def bc(ap, shape):
            return ap.unsqueeze(1).broadcast_to(shape)

        const_in, ident_zero, bias_ps, const_vec = (
            nc.alloc_semaphore(n) for n in ("const_in", "ident_zero", "bias_ps", "const_vec"))
        with nc.Block() as block:
            @block.sync
            def _(sp):
                for k, w in (*w0.items(), *w1.items()):
                    sp.dma_start(w[:, :, :], a["W" + k].rearrange("(c p) n -> p c n", p=P)).then_inc(const_in, 16)
                sp.dma_start(wd[:, :, :], a["Wd"][0:D, :].rearrange("(c p) n -> p c n", p=P)).then_inc(const_in, 16)
                sp.dma_start(cols[:, :, :], a["columns"]).then_inc(const_in, 16)
                for k, r in row.items():
                    sp.dma_start(r[:, :], a[k].partition_broadcast(P)).then_inc(const_in, 16)

            @block.vector
            def _(dve):
                dve.memset(more_any[:, :], -float(B * ALL_01))
                dve.memset(minus_half[:, :], -0.5)
                for g in range(G):
                    dve.memset(kst[g][SROW:SROW + 1, :, :].bitcast(F32), 1.0)
                dve.wait_ge(const_in, 16 * N_CONST)
                dve.tensor_scalar(col["bq"][:, :], col["bq"][:, :], SCALE, None, ALU.mult)
                for k in "rz":
                    dve.tensor_tensor(col[f"b{k}i"][:, :], col[f"b{k}i"][:, :], col[f"b{k}h"][:, :], ALU.add).then_inc(const_vec, 1)
                dve.wait_ge(const_vec, 2)
                for k in "rz":
                    dve.tensor_scalar(col[f"b{k}i"][:, :], col[f"b{k}i"][:, :], 0.5, None, ALU.mult)

                dve.wait_ge(bias_ps, 1)
                dve.tensor_tensor(row["bo"][:, :], row["bo"][:, :], GB[0][:, 0:D], ALU.add)

            @block.tensor
            def _(pe):
                pe.wait_ge(const_in, 16 * N_CONST)
                for c in range(DC):
                    last = pe.matmul(GB[0][:, 0:D], col["bv"][:, c:c + 1].broadcast_to([P, P]), w0["o"][:, c, :],
                                     start=(c == 0), stop=(c == DC - 1))
                last.then_inc(bias_ps, 1)

            @block.gpsimd
            def _(pool):
                pool.memset(ident[:, :], 0.0).then_inc(ident_zero, 1)
                pool.memset(ones[:, :], 1.0)
                pool.memset(half_power[:, :], -0.5)
                pool.wait_ge(ident_zero, 1)
                pool.affine_select(out=ident[:, :], in_=ident[:, :], compare_op=ALU.not_equal, fill=1.0, base=0,
                                   pattern=[[-1, P]], channel_multiplier=1)

        nc.clear_and_free_semaphores([const_in, ident_zero, bias_ps, const_vec])
        nc.all_engine_barrier()

        def step(b, update, prepare, before=0, after=0, general=0):
            s = {n: nc.alloc_semaphore(f"{n}_{update}{prepare}{before}{general}") for n in names}
            attend = update and not general
            labels = LABELS if general else 1

            ctx_step = ExitStack()
            block = ctx_step.enter_context(nc.Block())

            @block.sync
            def _(sp):
                def move_part(g, k):
                    stack = (qst, kst)[k][g]
                    part = 2 * g + k + 1
                    hi, lo = highs_r[k], lows_r[k]
                    sp.wait_ge(s["hi_made"], 2 * part)
                    sp.wait_ge(s["lo_made"], 2 * part)
                    for h in range(GH):
                        for r, src in ((0, hi), (1, (lo, hi)[k]), (2, (hi, lo)[k])):
                            sp.dma_start(stack[r * HD:(r + 1) * HD, h, :].bitcast(F32),
                                         src[h * HD:(h + 1) * HD, :].bitcast(F32)).then_inc(s[f"stack_moved{g}{k}"], 16)

                def load_xT(b):
                    sp.dma_start(xT[:, :, :], a["xT"][b].rearrange("(c p) n -> p c n", p=P)).then_inc(s["xT_in"], 16)

                def load_adj(n, i):
                    if i > 1:
                        sp.wait_ge(s["bias_made"], i - 1)
                    sp.dma_start(adj_n[i % 2][:, :], a["adj"][n, i * P:(i + 1) * P, :]).then_inc(s[f"adjn_in{i % 2}"], 16)

                def load_adjT(n, i):
                    if i == 0:
                        for k in range(2):
                            sp.wait_ge(s[f"stack_moved1{k}"], 16 * 12)
                    if i == 1:
                        if update:
                            sp.wait_ge(s["agg_ps"], 4)
                    if i >= 4:
                        sp.wait_ge(s["more_read"], i - 3)
                    sp.dma_start(adj_t[i % 4], a["adjT"][n, i * P:(i + 1) * P, :]).then_inc(s[f"adjt_in{i % 4}"], 16)

                def phase_a(b, more_to_come):
                    sp.dma_start(x1[:, :, :], a["x"][b].rearrange("(t p) d -> p t d", p=P)).then_inc(s["x1_in"], 16)
                    if more_to_come:
                        load_xT(b + 1)
                        for i in range(2):
                            load_adj(b + 1, i)
                        sp.wait_ge(s["st_ps"], PAIRS // 2)
                        for k in range(2):
                            move_part(0, k)
                        sp.wait_ge(s["st_ps"], PAIRS)
                        for k in range(2):
                            move_part(1, k)

                def phase_b(b, update, prepare):
                    if not prepare:
                        return
                    n = b + 1
                    if not update:
                        load_xT(0)
                        for i in range(2):
                            load_adj(0, i)
                        for g in range(G):
                            for k in range(2):
                                move_part(g, k)
                    for i in range(2, 7):
                        load_adj(n, i)
                    for i in range(4):
                        load_adjT(n, i)
                    load_adj(n, 7)
                    for i in range(4, NT):
                        load_adjT(n, i)
                    sp.wait_ge(s["shift_sb"], 1)
                    sp.dma_start(shift_dram, shift[:, :]).then_inc(s["shift_out"], 16)
                    sp.wait_ge(s["shift_out"], 16)
                    for g in range(G):
                        sp.dma_start(qst[g][SROW:SROW + 1, :, :].bitcast(F32),
                                     shift_dram[g * GH * NT:(g + 1) * GH * NT, :].rearrange("(o h t) n -> o h (t n)", o=1, h=GH)
                                     ).then_inc(s["shift_moved"], 16)

                def load_labels():
                    sp.dma_start(x1[:, :, :], x1_dram[b].rearrange("(t p) d -> p t d", p=P)).then_inc(s["x1_in"], 16)
                    sp.dma_start(label_wd, a["Wd"].rearrange("(k p) n -> p k n", p=P)).then_inc(s["wd_in"], 16)
                    for mh in range(NH):
                        if mh > 0:
                            sp.wait_ge(s["mask_made"], 2 * LABELS * mh)
                        for e in range(2):
                            sp.dma_start(label_adj[e], a["adjT"][b, e * N // 2:(e + 1) * N // 2, mh * HALF:(mh + 1) * HALF]
                                         .rearrange("(k p) n -> p k n", p=P)).then_inc(s["labels_in"], 16)

                if general:
                    load_labels()
                elif update:
                    phase_a(b, prepare)
                phase_b(b, update, prepare)
                if prepare:
                    sp.wait_ge(s["shift_moved"], 32)

            @block.tensor
            def _(pe):
                def project(n, i):
                    g, k, nh = i // 4, i // 2 % 2, i % 2
                    if i == 0:
                        pe.wait_ge(s["xT_in"], 16)
                    if i > 0:
                        pe.wait_ge(s["proj_sb"], i)
                    for c in range(DC):
                        last = pe.matmul(GB[2][:, :], w0["qk"[k]][:, c, g * P:(g + 1) * P],
                                         xT[:, c, nh * HALF:(nh + 1) * HALF], start=(c == 0), stop=(c == DC - 1))
                    last.then_inc(s["proj_ps"], 1)

                def values(n, i):
                    if i == 0:
                        pe.wait_ge(s["proj_sb"], 8)
                        if update:
                            pe.wait_ge(s["rec_sb"], 4)
                    if i >= 2:
                        pe.wait_ge(s["vals_sb"], i - 1)
                    for t in range(2):
                        for c in range(DC):
                            last = pe.matmul(GB[2 + i % 2][:, t * D:(t + 1) * D], xT[:, c, (2 * i + t) * P:(2 * i + t + 1) * P],
                                             w0["v"][:, c, :], start=(c == 0), stop=(c == DC - 1))
                    last.then_inc(s["vals_ps"], 1)

                def finish(f, banks):
                    for k, bank in enumerate(banks):
                        for t in range(2):
                            for oh in range(DC):
                                last = pe.transpose(GB[bank][:, t * D + oh * P:t * D + (oh + 1) * P],
                                                    nT[:, oh, (2 * k + t) * P:(2 * k + t + 1) * P], ident[:, :])
                        last.then_inc(s["fin_ps"], 1)

                def phase_a(b, more_to_come):
                    for q in range(QUARTERS * NT + LAG):
                        j, t = q // NT, q % NT
                        if j < QUARTERS:
                            g, nh = j // NH, j % NH
                            for hp in range(2):
                                p = 2 * q + hp
                                if p >= 2:
                                    pe.wait_ge(s["prob_made"], p - 1)
                                for e in range(2):
                                    h = 2 * hp + e
                                    last = pe.matmul(SP[p % 2][:, e * HALF:(e + 1) * HALF],
                                                     kst[g][0:SROW + 1, h, t * P:(t + 1) * P],
                                                     qst[g][0:SROW + 1, h, nh * HALF:(nh + 1) * HALF],
                                                     start=True, stop=True)
                                last.then_inc(s["st_ps"], 1)
                        if q >= LAG:
                            w = q - LAG
                            k, tw = w // NT, w % NT
                            pe.wait_ge(s["prob_masked"], 2 * (w + 1))
                            if tw == 0 and k >= 2:
                                pe.wait_ge(s["att_sb"], k - 1)
                            if tw == 0 and k == 1 and before:
                                pe.wait_ge(s["fin_normed"], 4)
                            for h in range(GH):
                                f = k // NH * P + h * HD
                                last = pe.matmul(GB[k % 2][h * HD:(h + 1) * HD, :], vals[:, tw, f:f + HD],
                                                 probs[w % PSLOTS][:, h, :], start=(tw == 0), stop=(tw == NT - 1))
                            last.then_inc(s["pv_done"], 1)
                        if t == 4:
                            if j > 0:
                                pe.wait_ge(s["rec_sb"], j)
                            for i in range(4):
                                for h in range(GH):
                                    last = pe.matmul(GB[3][h * HD:(h + 1) * HD, i * P:(i + 1) * P],
                                                     recsum[:, g * GH + h, nh * 4 + i:nh * 4 + i + 1].broadcast_to([P, HD]),
                                                     ident[:, :], start=True, stop=True)
                            last.then_inc(s["rec_ps"], 1)
                        if before and q == 3:
                            finish(0, (1, 2))
                        if more_to_come and q in PROJECT_AT:
                            if q == PROJECT_AT[0] and before:
                                pe.wait_ge(s["fin_normed"], 4)
                            project(b + 1, PROJECT_AT.index(q))

                def turn_x1(mh):
                    for dh in range(DC):
                        for t in range(4):
                            last = pe.transpose(GB[2 * mh + dh][:, t * P:(t + 1) * P], x1[:, 4 * mh + t, dh * P:(dh + 1) * P], ident[:, :])
                        last.then_inc(s["x1T_ps"], 1)

                def phase_b(b, update, prepare):
                    n = b + 1
                    done = [0]

                    def score_tiles(count):
                        if not prepare:
                            return
                        for u in range(done[0], done[0] + count):
                            t, h = u // H, u % H
                            if u == 0:
                                for part in ("00", "01", "10"):
                                    pe.wait_ge(s[f"stack_moved{part}"], 16 * 12)
                                if update:
                                    pe.wait_ge(s["prob_made"], PAIRS)
                            if u == GH:
                                pe.wait_ge(s["stack_moved11"], 16 * 12)
                            if u >= 2:
                                pe.wait_ge(s["score_sb"], u - 1)
                            for mh in range(NH):
                                last = pe.matmul(SP[u % 2][:, mh * HALF:(mh + 1) * HALF],
                                                 qst[h // GH][0:KROWS, h % GH, t * P:(t + 1) * P],
                                                 kst[h // GH][0:KROWS, h % GH, mh * HALF:(mh + 1) * HALF],
                                                 start=True, stop=True)
                            last.then_inc(s["score_ps"], 1)
                        done[0] += count

                    if not update:
                        for i in range(8):
                            project(n, i)
                    for i in range(4):
                        if attend:
                            if i == 0:
                                pe.wait_ge(s["att_sb"], 4)
                            if i >= 2:
                                pe.wait_ge(s["y_sum"], i - 1)
                            for t in range(2):
                                for c in range(DC):
                                    last = pe.matmul(GB[i % 2][:, t * D:(t + 1) * D], hT[:, c, (2 * i + t) * P:(2 * i + t + 1) * P],
                                                     w0["o"][:, c, :], start=(c == 0), stop=(c == DC - 1))
                            last.then_inc(s["y_ps"], 1)
                        if i > 0:
                            score_tiles(1)
                            if prepare:
                                values(n, i - 1)
                    score_tiles(1)
                    if prepare:
                        values(n, 3)
                    score_tiles(8)
                    if attend:
                        pe.wait_ge(s["y_sum"], 4)
                        for m in range(NT):
                            for k in range(NT):
                                last = pe.matmul(GB[0][:, 2 * m:2 * m + 2], edge[:, k, m * P:(m + 1) * P], ones[:, 0:2],
                                                 start=(k == 0), stop=(k == NT - 1))
                        last.then_inc(s["cnt_ps"], 1)
                    score_tiles(4)
                    if attend:
                        pe.wait_ge(s["recip_made"], 1)
                        for mh in range(NH):
                            for i in range(4):
                                last = pe.matmul(GB[mh][:, i * P:(i + 1) * P], counts[:, 4 * mh + i:4 * mh + i + 1].broadcast_to([P, P]),
                                                 ident[:, :], start=True, stop=True)
                            last.then_inc(s["recip_ps"], 1)
                    score_tiles(4)
                    if attend:
                        if prepare:
                            pe.wait_ge(s["vals_sb"], 4)
                        pe.wait_ge(s["x1c_made"], 2)
                        pe.wait_ge(s["x1b_made"], 2)
                    for mh in range(0 if general else NH):
                        cols = slice(mh * HALF, (mh + 1) * HALF)
                        if update and mh == 1:
                            pe.wait_ge(s["recip_sb"], 2)
                            turn_x1(0)
                        for dh in range(DC):
                            if update and mh == 1:
                                pe.wait_ge(s["agg_sb"], dh + 1)
                            for k in range(NT):
                                if update:
                                    for e, part in enumerate((x1a, x1b, x1c)):
                                        last = pe.matmul(GB[2 + dh][:, :], part[:, k, dh * P:(dh + 1) * P], edge[:, k, cols],
                                                         start=(k == 0 and e == 0), stop=(k == NT - 1 and e == 2))
                                if k in (0, 2, 4, 5, 7):
                                    score_tiles(1)
                            if update:
                                last.then_inc(s["agg_ps"], 1)
                    for mh in range(NH):
                        if update and mh == 0 and general:
                            pe.wait_ge(s["recip_made"], 2 * labels)
                            turn_x1(0)
                        score_tiles(1)
                        if update and mh == 0:
                            pe.wait_ge(s["agg_sb"], 4 * labels)
                        for oh in range(DC):
                            if update and mh == 1 and oh == 1:
                                pe.wait_ge(s["new_made"], 2)
                                pe.wait_ge(s["zt_made"], 2)
                                finish(before, (0, 1))
                            if attend:
                                if mh == 1:
                                    pe.wait_ge(s["x1T_sb"], 3 + oh)
                                for c in range(DC):
                                    last = pe.matmul(GB[2 + oh][:, :], wd[:, c, oh * P:(oh + 1) * P],
                                                     aggT[:, c, mh * HALF:(mh + 1) * HALF], start=(c == 0), stop=(c == DC - 1))
                                last.then_inc(s["wd_ps"], 1)
                            score_tiles(1)
                        for oh in range(DC):
                            q = 2 * mh + oh
                            o = slice(oh * P, (oh + 1) * P)
                            tiles = int(q < 3)

                            def products(bank, w, v, first, last):
                                if update:
                                    for c in range(DC):
                                        mm = pe.matmul(GB[bank][:, :], w1[w][:, c, o], v[:, c, :], start=(first and c == 0),
                                                       stop=(last and c == DC - 1))
                                    return mm

                            if update:
                                if oh == 0:
                                    pe.wait_ge(s["x1T_sb"], 2 * (mh + 1))
                                    if mh == 1:
                                        pe.wait_ge(s["out_sb"], 3)
                                if q > 0:
                                    pe.wait_ge(s["rt_made"], q)
                            products(R_BANK[mh], "rh", x1Ts[mh], True, False)
                            score_tiles(tiles)
                            if update:
                                pe.wait_ge(s["out_sb"], 2 * (mh + 1))
                                if q > 0:
                                    pe.wait_ge(s["nh_sb"], q)
                                products(3, "nh", x1Ts[mh], True, True).then_inc(s["nh_ps"], 1)
                            score_tiles(tiles)
                            if update:
                                products(R_BANK[mh], "ri", outT, False, True).then_inc(s["r_ps"], 1)
                            score_tiles(tiles)
                            if update:
                                if q > 0:
                                    pe.wait_ge(s["s_made"], q)
                                if q == 2:
                                    pe.wait_ge(s["fin_normed"], 4 * (before + 1))
                                products(NI_BANK[mh], "ni", outT, True, True).then_inc(s["ni_ps"], 1)
                            score_tiles(tiles)
                            if update and q > 0:
                                pe.wait_ge(s["zt_made"], q)
                            products(1, "zh", x1Ts[mh], True, False)
                            score_tiles(tiles)
                            if q == 2:
                                score_tiles(1)
                            if update:
                                products(1, "zi", outT, False, True).then_inc(s["z_ps"], 1)
                                if q == 1:
                                    pe.wait_ge(s["s_made"], 2)
                                    turn_x1(1)
                            if mh == 0:
                                score_tiles(1)
                            if q == 2 and prepare:
                                pe.wait_ge(s["shift_rounded"], 1)
                                pe.transpose(SP[0][0:H * NT, 0:P], shift_r[:, :, :].bitcast(F32).rearrange("p h t -> p (h t)"),
                                             ident[:, :]).then_inc(s["shift_ps"], 1)
                        if mh == 1 and after:
                            pe.wait_ge(s["new_made"], 4)
                            finish(before + 1, (0, 1))

                def label_sums():
                    pe.wait_ge(s["x1_in"], 16)
                    pe.wait_ge(s["ones_made"], 1)
                    pe.wait_ge(s["wd_in"], 16)
                    for mh in range(NH):
                        for d in range(LABELS):
                            r = LABELS * mh + d
                            pe.wait_ge(s["mask_made"], 2 * (r + 1))
                            if r > 0:
                                pe.wait_ge(s["cnt_sum"], r)
                            for k in range(NT):
                                last = pe.matmul(GB[0][:, :], ones_f, label_mask[:, k, :], start=(k == 0), stop=(k == NT - 1))
                            last.then_inc(s["cnt_ps"], 1)
                            if r > 0:
                                pe.wait_ge(s["agg_sb"], DC * r)
                            for dh in range(DC):
                                for k in range(NT):
                                    last = pe.matmul(GB[2 + dh][:, :], x1[:, k, dh * P:(dh + 1) * P], label_mask[:, k, :],
                                                     start=(k == 0), stop=(k == NT - 1))
                                last.then_inc(s["agg_ps"], 1)
                            pe.wait_ge(s["agg_sb"], DC * (r + 1))
                            for oh in range(DC):
                                for c in range(DC):
                                    last = pe.matmul(SP[mh][:, oh * HALF:(oh + 1) * HALF], label_wd[:, DC * d + c, oh * P:(oh + 1) * P],
                                                     aggT[:, c, mh * HALF:(mh + 1) * HALF], start=(d == 0 and c == 0),
                                                     stop=(d == LABELS - 1 and c == DC - 1))
                                if d == LABELS - 1:
                                    last.then_inc(s["wd_ps"], 1)
                                elif oh == DC - 1:
                                    last.then_inc(s["wd_part"], 1)

                if general:
                    label_sums()
                elif update:
                    phase_a(b, prepare)
                phase_b(b, update, prepare)

            @block.scalar
            def _(act):
                def project(n, i):
                    g, k, nh = i // 4, i // 2 % 2, i % 2
                    act.wait_ge(s["proj_ps"], i + 1)
                    if g == 1 and nh == 0:
                        act.wait_ge(s[f"stack_moved0{k}"], 16 * 12)
                    act.activation(lows[k][:, nh * HALF:(nh + 1) * HALF], GB[2][:, :], ACT.Identity, bias=col[("bq", "bk")[k]][:, g:g + 1],
                                   scale=(SCALE, 1.0)[k]).then_inc(s["proj_sb"], 1)

                def finish_norm(banks):
                    act.wait_ge(s["shift2_made"], 1)
                    for t in range(4):
                        act.activation(final[:, t, :], GB[banks[t // 2]][:, t % 2 * D:(t % 2 + 1) * D], ACT.Identity,
                                       bias=shift2[:, t:t + 1], scale=rstd2[:, t:t + 1]).then_inc(s["fin_normed"], 1)

                def phase_a(b, more_to_come):
                    for j in range(QUARTERS):
                        for t in range(NT):
                            q = j * NT + t
                            if q >= PSLOTS:
                                act.wait_ge(s["pv_done"], q - PSLOTS + 1)
                            for hp in range(2):
                                p = 2 * q + hp
                                act.wait_ge(s["st_ps"], p + 1)
                                act.activation(probs[q % PSLOTS][:, 2 * hp:2 * hp + 2, :],
                                               SP[p % 2][:, :].rearrange("p (h n) -> p h n", h=2), ACT.Exp).then_inc(s["prob_made"], 1)
                            if t == 5:
                                act.wait_ge(s["rec_ps"], j + 1)
                                if j > 0:
                                    act.wait_ge(s["att_sb"], j)
                                act.activation(recb[:, :], GB[3][:, :], ACT.Copy).then_inc(s["rec_sb"], 1)
                            if before and q == 7:
                                finish_norm((1, 2))
                            if more_to_come and q - 1 in PROJECT_AT:
                                project(b + 1, PROJECT_AT.index(q - 1))

                def phase_b(b, update, prepare):
                    n = b + 1
                    done = [0]

                    def score_tiles(count):
                        if not prepare:
                            return
                        for u in range(done[0], done[0] + count):
                            t, h = u // H, u % H
                            act.wait_ge(s["score_sb"], u + 1)
                            act.activation(scores[u % SLOTS][:, :], scores[u % SLOTS][:, :], ACT.Exp, scale=-1.0,
                                           bias=negmax[:, h, t:t + 1], accum_out=rowsum[:, h, t:t + 1]).then_inc(s["exp_made"], 1)
                        done[0] += count

                    def x1T_in(mh):
                        for dh in range(DC):
                            act.wait_ge(s["x1T_ps"], 2 * mh + dh + 1)
                            if mh == 1:
                                act.wait_ge(s["wd_ps"], 2)
                            act.activation(x1Ts[mh][:, dh, :], GB[2 * mh + dh][:, :], ACT.Copy).then_inc(s["x1T_sb"], 1)

                    def look_through(i):
                        if prepare:
                            act.wait_ge(s["edge_made"], i + 1)
                            act.activation(adj_t[i % 4], adj_t[i % 4], ACT.Square, bias=minus_half[:, :], accum_out=more[:, i:i + 1]).then_inc(s["more_read"], 1)

                    if not update:
                        for i in range(8):
                            project(n, i)
                    for i in range(4):
                        score_tiles(1)
                        if prepare:
                            act.wait_ge(s["vals_ps"], i + 1)
                            if i == 0 and update:
                                act.wait_ge(s["pv_done"], QUARTERS * NT)
                            act.activation(vals[:, 2 * i:2 * i + 2, :], GB[2 + i % 2][:, :].rearrange("p (t d) -> p t d", t=2),
                                           ACT.Copy).then_inc(s["vals_sb"], 1)
                    score_tiles(ACT_X1A)
                    for e in range(2):
                        half = slice(4 * e, 4 * e + 4)
                        if attend:
                            act.wait_ge(s["x1_made"], e + 1)
                            act.wait_ge(s["att_sb"], 4)
                            act.wait_ge(s["y_ps"], 4)
                            act.activation(x1a[:, half, :], x1[:, half, :], ACT.Copy).then_inc(s["x1a_made"], 1)
                        score_tiles((1, 3)[e])
                    for e in range(2):
                        half = slice(4 * e, 4 * e + 4)
                        if attend:
                            act.wait_ge(s["rest_made"], e + 1)
                            act.activation(x1b[:, half, :], rest[:, half, :], ACT.Copy).then_inc(s["x1b_made"], 1)
                        score_tiles((1, 18 - 9 - ACT_X1A)[e])
                    if attend:
                        for mh in range(NH):
                            act.wait_ge(s["recip_ps"], mh + 1)
                            act.activation(recip[:, mh * HALF:(mh + 1) * HALF], GB[mh][:, :], ACT.Copy).then_inc(s["recip_sb"], 1)
                    score_tiles(14)
                    if attend:
                        x1T_in(0)
                    score_tiles(8)
                    for mh in range(NH):
                        if update and mh == 0 and general:
                            x1T_in(0)
                        score_tiles(1)
                        for oh in range(DC):
                            if update:
                                act.wait_ge(s["wd_ps"], 2 * mh + oh + 1)
                                product = SP[mh][:, oh * HALF:(oh + 1) * HALF] if general else GB[2 + oh][:, :]
                                act.activation(outT[:, oh, :], product, ACT.Relu, bias=col["bd"][:, oh:oh + 1]).then_inc(s["out_sb"], 1)
                            score_tiles(1)
                        if mh == 0:
                            for i in range(3):
                                look_through(i)
                        for oh in range(DC):
                            q = 2 * mh + oh
                            tiles = int(q < 3)
                            score_tiles(2 * tiles)
                            if update:
                                act.wait_ge(s["nh_ps"], q + 1)
                                if q >= 2:
                                    act.wait_ge(s["fin_ps"], 2 * (before + 1))
                                act.activation(nT[:, oh, :], GB[3][:, :], ACT.Identity, bias=col["bnh"][:, oh:oh + 1]).then_inc(s["nh_sb"], 1)
                                act.wait_ge(s["r_ps"], q + 1)
                                if q == 0 and not general:
                                    act.wait_ge(s["x1c_made"], 2)
                                act.activation(rT[:, oh, :], GB[R_BANK[mh]][:, :], ACT.Tanh, bias=col["bri"][:, oh:oh + 1], scale=0.5).then_inc(s["rt_made"], 1)
                            score_tiles(tiles)
                            if mh == 0:
                                look_through(3 + 2 * oh)
                            score_tiles(tiles)
                            if update:
                                act.wait_ge(s["s_made"], q + 1)
                                act.activation(nT[:, oh, :], nT[:, oh, :], ACT.Tanh, bias=col["bni"][:, oh:oh + 1]).then_inc(s["n_made"], 1)
                            score_tiles(tiles)
                            if mh == 0:
                                look_through(4 + 2 * oh)
                            if q == 2:
                                score_tiles(1)
                            if update:
                                act.wait_ge(s["z_ps"], q + 1)
                                act.activation(zT[:, oh, :], GB[1][:, :], ACT.Tanh, bias=col["bzi"][:, oh:oh + 1], scale=0.5).then_inc(s["zt_made"], 1)
                                if q == 1:
                                    x1T_in(1)
                            if mh == 0:
                                score_tiles(1)
                            if q == 1:
                                look_through(7)
                            if q == 2 and prepare:
                                act.wait_ge(s["excess_made"], 1)
                                act.activation(excess[:, :, :], excess[:, :, :], ACT.Exp).then_inc(s["excess_exp"], 1)
                if attend:
                    phase_a(b, prepare)
                phase_b(b, update, prepare)

            @block.vector
            def _(dve):
                def high_part(n, i):
                    g, k, nh = i // 4, i // 2 % 2, i % 2
                    cols = slice(nh * HALF, (nh + 1) * HALF)
                    dve.wait_ge(s["proj_sb"], i + 1)
                    dve.tensor_copy(highs_r[k][:, cols], lows[k][:, cols]).then_inc(s["hi_made"], 1)

                def finish_stats(f, banks):
                    for k, bank in enumerate(banks):
                        dve.wait_ge(s["fin_ps"], 2 * f + k + 1)
                        if f + k > 0:
                            dve.wait_ge(s["mv2_made"], 4 * f + 2 * k)
                        for t in range(2):
                            dve.bn_stats(stats2[:, t, :], GB[bank][:, t * D:(t + 1) * D]).then_inc(s["st2_made"], 1)
                        for t in range(2):
                            dve.wait_ge(s["st2_made"], 4 * f + 2 * k + t + 1)
                            dve.bn_aggr(mv2[:, 2 * k + t, :], stats2[:, t, :]).then_inc(s["mv2_made"], 1)

                def finish_norm(f, banks):
                    dve.wait_ge(s["rstd2_made"], f + 1)
                    if f > 0:
                        dve.wait_ge(s["fin_saved"], 16 * f)
                    for t in range(4):
                        dve.tensor_scalar(final[:, t, :], GB[banks[t // 2]][:, t % 2 * D:(t % 2 + 1) * D], mv2[:, t, 0:1],
                                          rstd2[:, t:t + 1], ALU.subtract, ALU.mult).then_inc(s["fin_normed"], 1)

                def phase_a(b, more_to_come):
                    def normalise(j):
                        g, nh = j // NH, j % NH
                        dve.wait_ge(s["pv_done"], NT * (j + 1))
                        dve.wait_ge(s["rec_sb"], j + 1)
                        dve.tensor_tensor(hT[:, g, nh * HALF:(nh + 1) * HALF], GB[j % 2][:, :], recb[:, :], ALU.mult).then_inc(s["att_sb"], 1)

                    for j in range(QUARTERS):
                        for t in range(NT):
                            for hp in range(2):
                                p = (j * NT + t) * 2 + hp
                                dve.wait_ge(s["prob_made"], p + 1)
                                tile = probs[(j * NT + t) % PSLOTS][:, 2 * hp:2 * hp + 2, :]
                                dve.tensor_tensor(tile, tile, bc(edge[:, t, j % NH * HALF:(j % NH + 1) * HALF], [P, 2, HALF]),
                                                  ALU.min).then_inc(s["prob_masked"], 1)
                            if j > 0 and t == 3:
                                normalise(j - 1)
                            if before and j == 0 and t == 4:
                                finish_stats(0, (1, 2))
                            if more_to_come and j * NT + t - 2 in PROJECT_AT:
                                high_part(b + 1, PROJECT_AT.index(j * NT + t - 2))
                    normalise(QUARTERS - 1)

                def phase_b(b, update, prepare):
                    n = b + 1
                    done = [0]

                    def score_tiles(count):
                        if not prepare:
                            return
                        for u in range(done[0], done[0] + count):
                            t, h = u // H, u % H
                            if h == 0:
                                dve.wait_ge(s[f"adjn_in{t % 2}"], 16 * (t // 2 + 1))
                                if u > H:
                                    dve.wait_ge(s["score_sb"], u - H)
                                dve.tensor_scalar(bias[t % 2][:, :], adj_n[t % 2][:, :], 0.0, NOEDGE,
                                                  ALU.is_equal, ALU.mult).then_inc(s["bias_made"], 1)
                                dve.wait_ge(s["bias_made"], t + 1)
                            dve.wait_ge(s["score_ps"], u + 1)
                            if u >= SLOTS:
                                dve.wait_ge(s["exp_made"], u - SLOTS + 1)
                            dve.tensor_tensor_reduce(out=scores[u % SLOTS][:, :], in0=SP[u % 2][:, :], in1=bias[t % 2][:, :],
                                                     scale=-1.0, scalar=-NEG_INF, op0=ALU.add, op1=ALU.min,
                                                     accum_out=negmax[:, h, t:t + 1]).then_inc(s["score_sb"], 1)
                        done[0] += count

                    def combine(q):
                        oh = q % 2
                        dve.wait_ge(s["n_made"], q + 1)
                        dve.tensor_tensor(rT[:, oh, :], x1Ts[q // 2][:, oh, :], nT[:, oh, :], ALU.subtract).then_inc(s["diff_made"], 1)
                        dve.wait_ge(s["diff_made"], q + 1)
                        dve.wait_ge(s["zt_made"], q + 1)
                        dve.scalar_tensor_tensor(rT[:, oh, :], zT[:, oh, :], 1.0, rT[:, oh, :], ALU.add, ALU.mult).then_inc(s["prod_made"], 1)
                        dve.wait_ge(s["prod_made"], q + 1)
                        dve.scalar_tensor_tensor(nT[:, oh, :], rT[:, oh, :], 0.5, nT[:, oh, :], ALU.mult, ALU.add).then_inc(s["new_made"], 1)

                    def edges(i):
                        if prepare:
                            dve.wait_ge(s[f"adjt_in{i % 4}"], 16 * (i // 4 + 1))
                            if i == 0:
                                if update:
                                    dve.wait_ge(s["agg_ps"], 4)
                                if update:
                                    dve.wait_ge(s["cnt_ps"], 1)
                            dve.tensor_scalar(edge[:, i, :], adj_t[i % 4], 0.0, EDGE, ALU.not_equal, ALU.mult).then_inc(s["edge_made"], 1)

                    if not update:
                        for i in range(8):
                            high_part(n, i)
                    for i in range(4):
                        if attend:
                            two = slice(2 * i, 2 * i + 2)
                            if i == 0:
                                dve.wait_ge(s["biased"], 1)
                            dve.wait_ge(s["y_ps"], i + 1)
                            dve.tensor_tensor(x1[:, two, :], GB[i % 2][:, :].rearrange("p (t d) -> p t d", t=2), x1[:, two, :],
                                              ALU.add).then_inc(s["y_sum"], 1)
                            dve.wait_ge(s["y_sum"], i + 1)
                            if i > 0:
                                dve.wait_ge(s["mv_made"], 2 * i)
                            for t in range(2):
                                dve.bn_stats(stats[:, t, :], x1[:, 2 * i + t, :]).then_inc(s["stats_made"], 1)
                            for t in range(2):
                                dve.wait_ge(s["stats_made"], 2 * i + t + 1)
                                dve.bn_aggr(mv[:, 2 * i + t, :], stats[:, t, :]).then_inc(s["mv_made"], 1)
                        if i > 0:
                            score_tiles(1)
                    score_tiles(1)
                    if attend:
                        dve.wait_ge(s["rstd_made"], 1)
                        for i in range(NT):
                            dve.tensor_scalar(x1[:, i, :], x1[:, i, :], mv[:, i, 0:1], rstd[:, i:i + 1],
                                              ALU.subtract, ALU.mult).then_inc(s["normed"], 1)
                    score_tiles(10)
                    if attend:
                        dve.wait_ge(s["cnt_ps"], 1)
                        dve.tensor_scalar(counts[:, :], GB[0][:, 0:2 * NT:2], EDGE * EPS_COUNT, None, ALU.add).then_inc(s["cnt_sum"], 1)
                        dve.wait_ge(s["cnt_sum"], 1)
                        dve.reciprocal(counts[:, :], counts[:, :]).then_inc(s["recip_made"], 1)
                    score_tiles(6)
                    for mh in range(0 if general else NH):
                        for dh in range(DC):
                            score_tiles(5)
                            if update:
                                dve.wait_ge(s["agg_ps"], 2 * mh + dh + 1)
                                dve.wait_ge(s["recip_sb"], mh + 1)
                                dve.tensor_tensor(aggT[:, dh, mh * HALF:(mh + 1) * HALF], GB[2 + dh][:, :],
                                                  recip[:, mh * HALF:(mh + 1) * HALF],
                                                  ALU.mult).then_inc(s["agg_sb"], 1)
                    for mh in range(NH):
                        score_tiles(1)
                        if mh == 0:
                            edges(0)
                            for oh in range(DC):
                                score_tiles(1)
                                edges(1 + oh)
                        else:
                            if update:
                                finish_stats(before, (0, 1))
                            score_tiles(1)
                            if update:
                                finish_norm(before, (0, 1))
                            score_tiles(1)
                        for oh in range(DC):
                            q = 2 * mh + oh
                            tiles = int(q < 3)
                            score_tiles(tiles)
                            score_tiles(tiles)
                            if update and oh == 1:
                                combine(q - 1)
                            score_tiles(tiles)
                            if update:
                                dve.wait_ge(s["rt_made"], q + 1)
                                dve.wait_ge(s["nh_sb"], q + 1)
                                dve.scalar_tensor_tensor(nT[:, oh, :], rT[:, oh, :], 1.0, nT[:, oh, :],
                                                         ALU.add, ALU.mult).then_inc(s["t_made"], 1)
                            if mh == 0:
                                edges(3 + 2 * oh)
                            score_tiles(tiles)
                            if update:
                                dve.wait_ge(s["ni_ps"], q + 1)
                                dve.wait_ge(s["t_made"], q + 1)
                                dve.scalar_tensor_tensor(nT[:, oh, :], nT[:, oh, :], 0.5, GB[NI_BANK[mh]][:, :],
                                                         ALU.mult, ALU.add).then_inc(s["s_made"], 1)
                            if mh == 0:
                                edges(4 + 2 * oh)
                            score_tiles((1 + mh) * tiles)
                            if q == 2 and prepare:
                                dve.wait_ge(s["score_sb"], TILES)
                                dve.tensor_copy(shift_r[:, :, :], negmax[:, :, :]).then_inc(s["shift_rounded"], 1)
                                dve.wait_ge(s["shift_rounded"], 1)
                                dve.tensor_tensor(excess[:, :, :], shift_r[:, :, :].bitcast(F32), negmax[:, :, :],
                                                  ALU.subtract).then_inc(s["excess_made"], 1)
                            if mh == 0:
                                score_tiles(1)
                            if q == 1:
                                edges(7)
                            if q == 2 and prepare:
                                dve.wait_ge(s["shift_ps"], 1)
                                dve.tensor_copy(shift[:, :], SP[0][0:H * NT, 0:P]).then_inc(s["shift_sb"], 1)
                        if update:
                            combine(2 * mh + 1)
                        if mh == 1 and prepare:
                            dve.wait_ge(s["exp_made"], TILES)
                            dve.wait_ge(s["excess_exp"], 1)
                            dve.tensor_tensor(rowsum[:, :, :], rowsum[:, :, :], excess[:, :, :], ALU.mult).then_inc(s["sum_shifted"], 1)
                            dve.wait_ge(s["sum_shifted"], 1)
                            if update:
                                dve.wait_ge(s["rec_ps"], 4)
                            dve.reciprocal(recsum[:, :, :], rowsum[:, :, :]).then_inc(s["recsum_made"], 1)
                            dve.wait_ge(s["more_read"], NT)
                            dve.tensor_tensor(more_any[:, :], more_any[:, :], more[:, :], ALU.add).then_inc(s["more_made"], 1)
                        if mh == 1 and after:
                            finish_stats(before + 1, (0, 1))
                            finish_norm(before + 1, (0, 1))

                def label_masks():
                    dve.memset(ones_f, 1.0).then_inc(s["ones_made"], 1)
                    for mh in range(NH):
                        for d in range(LABELS):
                            r = LABELS * mh + d
                            dve.wait_ge(s["labels_in"], 32 * (mh + 1))
                            if r > 0:
                                dve.wait_ge(s["agg_ps"], DC * r)
                            if r > 0:
                                dve.wait_ge(s["cnt_ps"], r)
                            for e in range(2):
                                dve.tensor_scalar(label_mask[:, e * NT // 2:(e + 1) * NT // 2, :], label_adj[e], float(d + 1), None,
                                                  ALU.is_equal).then_inc(s["mask_made"], 1)
                            dve.wait_ge(s["cnt_ps"], r + 1)
                            if r > 0:
                                dve.wait_ge(s["agg_sb"], DC * r)
                            dve.tensor_scalar(recip[:, 0:HALF], GB[0][:, :], EPS_COUNT, None, ALU.add).then_inc(s["cnt_sum"], 1)
                            dve.wait_ge(s["cnt_sum"], r + 1)
                            dve.reciprocal(recip[:, 0:HALF], recip[:, 0:HALF]).then_inc(s["recip_made"], 1)
                            dve.wait_ge(s["recip_made"], r + 1)
                            if d > 0:
                                dve.wait_ge(s["wd_part"], (LABELS - 1) * mh + d)
                            for dh in range(DC):
                                dve.wait_ge(s["agg_ps"], DC * r + dh + 1)
                                dve.tensor_tensor(aggT[:, dh, mh * HALF:(mh + 1) * HALF], GB[2 + dh][:, :], recip[:, 0:HALF],
                                                  ALU.mult).then_inc(s["agg_sb"], 1)

                if general:
                    label_masks()
                elif update:
                    phase_a(b, prepare)
                phase_b(b, update, prepare)

            @block.gpsimd
            def _(pool):
                def low_part(n, i):
                    g, k, nh = i // 4, i // 2 % 2, i % 2
                    cols = slice(nh * HALF, (nh + 1) * HALF)
                    pool.wait_ge(s["hi_made"], i + 1)
                    pool.tensor_tensor(lows_r[k][:, cols], lows[k][:, cols], highs_r[k][:, cols].bitcast(F32),
                                       ALU.subtract).then_inc(s["lo_made"], 1)

                def finish(f, b, mh):
                    pool.wait_ge(s["mv2_made"], 4 * (f + 1))
                    pool.tensor_scalar(small2[:, :], mv2[:, :, 1], EPS0, None, ALU.add).then_inc(s["eps2_added"], 1)
                    pool.wait_ge(s["eps2_added"], f + 1)
                    pool.tensor_tensor(rstd2[:, :], small2[:, :], half_power[:, 0:4], ALU.pow).then_inc(s["rstd2_made"], 1)
                    if mh == 1 and before and f == 0:
                        pool.wait_ge(s["rstd2_made"], 1)
                        pool.tensor_tensor(small2[:, :], mv2[:, :, 0], rstd2[:, :], ALU.mult).then_inc(s["scaled_mean2"], 1)
                        pool.wait_ge(s["scaled_mean2"], 1)
                        pool.tensor_scalar(shift2[:, :], small2[:, :], -1.0, None, ALU.mult).then_inc(s["shift2_made"], 1)
                    pool.wait_ge(s["fin_normed"], 4 * (f + 1))
                    pool.tensor_tensor(final[:, :, :], final[:, :, :], bc(row["g1"][:, :], [P, 4, D]), ALU.mult).then_inc(s["fin_scaled"], 1)
                    pool.wait_ge(s["fin_scaled"], f + 1)
                    pool.tensor_tensor(final[:, :, :], final[:, :, :], bc(row["b1"][:, :], [P, 4, D]), ALU.add).then_inc(s["fin_made"], 1)
                    pool.wait_ge(s["fin_made"], f + 1)
                    pool.dma_start(out[b, mh * HALF:(mh + 1) * HALF, :].rearrange("(t p) d -> p t d", p=P),
                                   final[:, :, :]).then_inc(s["fin_saved"], 16)

                def phase_a(b, more_to_come):
                    pool.wait_ge(s["x1_in"], 16)
                    pool.tensor_tensor(x1[:, :, :], x1[:, :, :], bc(row["bo"][:, :], [P, NT, D]), ALU.add).then_inc(s["biased"], 1)
                    if before:
                        finish(0, b - 1, 1)
                    if more_to_come:
                        for i in range(8):
                            low_part(b + 1, i)

                def split_x1(b):
                    pool.wait_ge(s["mv_made"], NT)
                    pool.tensor_scalar(small[:, :], mv[:, :, 1], EPS0, None, ALU.add).then_inc(s["eps_added"], 1)
                    pool.wait_ge(s["eps_added"], 1)
                    pool.tensor_tensor(rstd[:, :], small[:, :], half_power[:, :], ALU.pow).then_inc(s["rstd_made"], 1)
                    for e in range(2):
                        half = slice(4 * e, 4 * e + 4)
                        pool.wait_ge(s["normed"], 4 * (e + 1))
                        pool.tensor_tensor(x1[:, half, :], x1[:, half, :], bc(row["g0"][:, :], [P, 4, D]), ALU.mult).then_inc(s["scaled"], 1)
                        pool.wait_ge(s["scaled"], e + 1)
                        pool.tensor_tensor(x1[:, half, :], x1[:, half, :], bc(row["b0"][:, :], [P, 4, D]), ALU.add).then_inc(s["x1_made"], 1)
                    for e in range(2):
                        half = slice(4 * e, 4 * e + 4)
                        pool.wait_ge(s["x1a_made"], e + 1)
                        pool.wait_ge(s["pv_done"], QUARTERS * NT)
                        pool.tensor_tensor(rest[:, half, :], x1[:, half, :], x1a[:, half, :], ALU.subtract).then_inc(s["rest_made"], 1)
                    for e in range(2):
                        half = slice(4 * e, 4 * e + 4)
                        pool.wait_ge(s["x1b_made"], e + 1)
                        if prepare:
                            for k in range(2):
                                pool.wait_ge(s[f"stack_moved1{k}"], 16 * 12)
                        pool.tensor_tensor(x1c[:, half, :], rest[:, half, :], x1b[:, half, :], ALU.subtract).then_inc(s["x1c_made"], 1)
                    pool.wait_ge(s["x1_made"], 2)
                    pool.dma_start(x1_dram[b].rearrange("(t p) d -> p t d", p=P), x1[:, :, :]).then_inc(s["x1_saved"], 16)

                def phase_b(b, update, prepare):
                    n = b + 1
                    if not update:
                        for i in range(8):
                            low_part(n, i)
                    if not update:
                        return
                    if not general:
                        split_x1(b)
                    for mh in range(NH):
                        if mh == 0 or after:
                            finish(before + mh, b, mh)

                if attend:
                    phase_a(b, prepare)
                phase_b(b, update, prepare)
                if update:
                    pool.wait_ge(s["fin_saved"], 16 * (before + 1 + after))
                if attend:
                    pool.wait_ge(s["x1_saved"], 16)


            ctx_step.close()
            nc.clear_and_free_semaphores(list(s.values()))
            nc.all_engine_barrier()

        step(-1, 0, 1)
        step(0, 1, 1)
        with nc.Fori(1, B - 1) as b:
            step(b, 1, 1, before=1)
        step(B - 1, 1, 0, before=1, after=1)

        flag_made, flag_ps, flag_sb, flag_read = (nc.alloc_semaphore(n) for n in ("flag_made", "flag_ps", "flag_sb", "flag_read"))
        with nc.Block() as block:
            @block.vector
            def _(dve):
                dve.tensor_reduce(flag[:, :], more_any[:, :], AX.X, ALU.max).then_inc(flag_made, 1)
                dve.wait_ge(flag_made, 1)
                dve.tensor_scalar(flags[:, :], flag[:, :].broadcast_to([P, 2]), 0.0, None, ALU.is_gt).then_inc(flag_made, 1)
                dve.wait_ge(flag_ps, 1)
                dve.tensor_scalar(general_flag[:, :], SP[0][0:1, 0:1], 0.0, None, ALU.is_gt).then_inc(flag_sb, 1)

            @block.tensor
            def _(pe):
                pe.wait_ge(flag_made, 2)
                pe.matmul(SP[0][:, 0:2], ones[:, :], flags[:, :], start=True, stop=True).then_inc(flag_ps, 1)

        nc.clear_and_free_semaphores([flag_made, flag_ps, flag_sb, flag_read])
        nc.all_engine_barrier()
        general = nc.values_load(general_flag[0:1, 0:1], min_val=0, max_val=1)
        with nc.If(general > 0):
            with nc.Fori(0, B) as b:
                step(b, 1, 0, after=1, general=1)


_NAMES = {"Wq": "L0_gnn_Wq", "Wk": "L0_gnn_Wk", "Wv": "L0_gnn_Wv", "Wo": "L0_gnn_Wo",
          "bo": "L0_gnn_bo",
          "g0": "L0_gnn_gamma", "b0": "L0_gnn_beta", "g1": "L1_gnn_gamma", "b1": "L1_gnn_beta"}
_COLUMNS = ("L0_gnn_bv", "L0_gnn_bq", "L0_gnn_bk", "L1_gnn_bd", "L1_gnn_bri", "L1_gnn_brh", "L1_gnn_bzi",
            "L1_gnn_bzh", "L1_gnn_bni", "L1_gnn_bnh")
_TURNED = {"Wd": "L1_gnn_Wd", "Wri": "L1_gnn_Wri", "Wrh": "L1_gnn_Wrh", "Wzi": "L1_gnn_Wzi",
           "Wzh": "L1_gnn_Wzh", "Wni": "L1_gnn_Wni", "Wnh": "L1_gnn_Wnh"}


def kernel(**inputs):
    import numpy as _np
    import concourse.bacc as _bacc
    from concourse import mybir as _mybir
    from concourse.bass_utils import run_bass_kernel_spmd as _run

    laid = {"x": _np.ascontiguousarray(inputs["x"]), "adj": _np.ascontiguousarray(inputs["adj"]),
            "xT": _np.ascontiguousarray(_np.asarray(inputs["x"]).transpose(0, 2, 1)),
            "adjT": _np.ascontiguousarray(_np.asarray(inputs["adj"]).transpose(0, 2, 1))}
    for k, v in _NAMES.items():
        laid[k] = _np.ascontiguousarray(inputs[v])
    for k, v in _TURNED.items():
        laid[k] = _np.ascontiguousarray(_np.asarray(inputs[v]).T)
    columns = _np.stack([_np.asarray(inputs[v]).reshape(DC, P) for v in _COLUMNS])
    laid["columns"] = _np.ascontiguousarray(columns.transpose(2, 0, 1))

    nc = _bacc.Bacc("TRN2", target_bir_lowering=False, num_devices=1)
    aps = {k: nc.dram_tensor(f"in_{k}", v.shape, _mybir.dt.from_np(v.dtype), kind="ExternalInput").ap()
           for k, v in laid.items()}
    out = nc.dram_tensor("out", (B, N, D), _mybir.dt.float32, kind="ExternalOutput").ap()
    graph_kernel(nc, aps, out)
    r = _run(nc, [{f"in_{k}": v for k, v in laid.items()}], core_ids=[0])
    return r.results[0]["out"]
```
